# Optimizing a Trainium2 kernel written in Bass

```python
import numpy as np
import jax
import jax.numpy as jnp

def _softmax(x, axis=-1):
    return jax.nn.softmax(x, axis=axis)

def _gelu(x):
    return jax.nn.gelu(x, approximate=True)

def _silu(x):
    return jax.nn.silu(x)

def _sigmoid(x):
    return jax.nn.sigmoid(x)

def _layernorm(x, axis=-1, eps=1e-05):
    m = jnp.mean(x, axis=axis, keepdims=True)
    v = jnp.var(x, axis=axis, keepdims=True)
    return (x - m) / jnp.sqrt(v + eps)

def _scatter_add(tgt, idx, src, axis=0):
    return tgt.at[idx].add(src)

def _segment_sum(src, seg, n):
    return jax.ops.segment_sum(src, seg, n)
kernel_name = 'mk_adj_preln_d1_adj_r2_421818'

def setup_inputs(seed: int=0):
    np.random.seed(seed)
    _w = jnp.asarray

    def _rec_inputs():
        import jax
        import jax.numpy as jnp
        _gk = jax.random.key(seed)
        x = 7.22e-05 + 1 * jax.random.normal(jax.random.fold_in(_gk, 1), (32, 256, 1024), jnp.float32)
        _w = (1.0 + jnp.arange(256, dtype=jnp.float32)) ** (-0.5)
        _w = _w / _w.mean()
        _pij = jnp.clip(0.015625 * _w[:, None] * _w[None, :], 0.0, 1.0)
        _a = jax.random.uniform(jax.random.fold_in(_gk, 2), (256, 256)) < _pij
        _a = jnp.logical_or(_a, jnp.swapaxes(_a, -1, -2))
        _a = jnp.logical_or(_a, jnp.eye(256, dtype=bool))
        _af = _a.astype(jnp.float32)
        _af = _af * jax.random.uniform(jax.random.fold_in(_gk, 3), (256, 256), jnp.float32, 0.05, 0.0885215)
        adj = _af
        return (x, adj)
    x, adj = _rec_inputs()

    def _L0_gnn_setup():
        import jax, jax.numpy as jnp
        import numpy as np
        B, S, N = (8, 256, 1024)
        HID = 256
        K = 8

        def _construct_adj(x, k):
            Bn, Sn, Nn = x.shape
            fv = x.mean(axis=1)
            nf = fv / jnp.linalg.norm(fv, axis=1, keepdims=True)
            sim = nf[:, :, None] * nf[:, None, :]
            kk = min(k, Nn - 1)
            _, idx = jax.lax.top_k(sim, kk + 1)
            idx = idx[..., 1:]
            b_ix = jnp.arange(Bn)[:, None, None]
            r_ix = jnp.arange(Nn)[None, :, None]
            adj = jnp.zeros((Bn, Nn, Nn), x.dtype).at[b_ix, r_ix, idx].set(1.0)
            adj = jnp.maximum(adj, jnp.swapaxes(adj, 1, 2))
            d = jnp.arange(Nn)
            adj = adj.at[:, d, d].set(1.0)
            return adj

        def _gc(x, adj, W, b):
            deg = adj.sum(axis=2, keepdims=True)
            deg = jnp.where(deg == 0, jnp.ones_like(deg), deg)
            h = x @ W.T + b
            return jnp.einsum('bij,bjh->bih', adj / deg, h)
        key = jax.random.key(seed)
        k0, k1, k2 = jax.random.split(key, 3)
        x = jax.random.normal(k0, (B, S, N), jnp.float32)
        W1 = jax.random.normal(k1, (HID, S), jnp.float32) * 0.02
        b1 = jnp.zeros((HID,), jnp.float32)
        W2 = jax.random.normal(k2, (S, HID), jnp.float32) * 0.02
        b2 = jnp.zeros((S,), jnp.float32)
        return {'x': x, 'W1': W1, 'b1': b1, 'W2': W2, 'b2': b2}
    _L0_gnn_all = _L0_gnn_setup()
    _L0_gnn_in = {k: v for k, v in _L0_gnn_all.items() if k in ('b1', 'b2')}
    del _L0_gnn_all
    return {'x': x, 'adj': adj, 'L0_gnn_b1': _L0_gnn_in['b1'], 'L0_gnn_b2': _L0_gnn_in['b2']}

def reference(x, adj, L0_gnn_b1, L0_gnn_b2):
    import jax
    import jax.numpy as jnp

    def _L0_gnn_ref(x, W1, b1, W2, b2):
        import jax, jax.numpy as jnp
        import numpy as np
        B, S, N = (8, 256, 1024)
        HID = 256
        K = 8

        def _construct_adj(x, k):
            Bn, Sn, Nn = x.shape
            fv = x.mean(axis=1)
            nf = fv / jnp.linalg.norm(fv, axis=1, keepdims=True)
            sim = nf[:, :, None] * nf[:, None, :]
            kk = min(k, Nn - 1)
            _, idx = jax.lax.top_k(sim, kk + 1)
            idx = idx[..., 1:]
            b_ix = jnp.arange(Bn)[:, None, None]
            r_ix = jnp.arange(Nn)[None, :, None]
            adj = jnp.zeros((Bn, Nn, Nn), x.dtype).at[b_ix, r_ix, idx].set(1.0)
            adj = jnp.maximum(adj, jnp.swapaxes(adj, 1, 2))
            d = jnp.arange(Nn)
            adj = adj.at[:, d, d].set(1.0)
            return adj

        def _gc(x, adj, W, b):
            deg = adj.sum(axis=2, keepdims=True)
            deg = jnp.where(deg == 0, jnp.ones_like(deg), deg)
            h = x @ W.T + b
            return jnp.einsum('bij,bjh->bih', adj / deg, h)
        adj = _construct_adj(x, K)
        xr = jnp.swapaxes(x, 1, 2)
        h = jax.nn.relu(_gc(xr, adj, W1, b1))
        h = _gc(h, adj, W2, b2)
        return jnp.swapaxes(h, 1, 2)
    h = jnp.maximum(_layernorm(x, axis=-1), 0.0)
    x = x + _L0_gnn_ref(h, adj, L0_gnn_b1, adj, L0_gnn_b2)
    return x

_drawn_inputs = setup_inputs


def setup_inputs(seed=0):
    import zlib

    import numpy as np

    out = dict(_drawn_inputs(seed))
    spreads = {'L0_gnn_b1': (0.0, 0.386), 'L0_gnn_b2': (0.0, 0.1)}
    factors = {}
    for name, (base, spread) in spreads.items():
        noise = np.random.default_rng([zlib.crc32(name.encode()), seed]).standard_normal(out[name].shape)
        drawn = base * np.exp(spread * noise) if base else spread * noise
        out[name] = jnp.asarray(drawn.astype(out[name].dtype))
    for name, factor in factors.items():
        out[name] = (out[name] * factor).astype(out[name].dtype)
    return out
```

```python
from contextlib import ExitStack

import concourse.bass as bass
from concourse import mybir

ALU = mybir.AluOpType
ACT = mybir.ActivationFunctionType
F32 = mybir.dt.float32

P = 128
TOP = 8
EPS = 1e-5


def gnn_kernel(nc, x, wT, b1, b2, ident_in, out):
    B, S, N = x.shape
    C = S // P
    T = N // P
    HALF = 512
    NH = N // HALF

    with ExitStack() as ctx:
        def sb(name, shape, dt=F32):
            return ctx.enter_context(nc.sbuf_tensor(name, shape, dt))

        def sem(name):
            return ctx.enter_context(nc.semaphore(name))

        ps_a = ctx.enter_context(nc.psum_tensor("ps_a", [P, 2048], F32))
        ps_b = ctx.enter_context(nc.psum_tensor("ps_b", [P, 2048], F32))

        w_t = sb("w_t", [P, C, S])
        bias1 = sb("bias1", [P, C])
        bias2 = sb("bias2", [P, C])
        ident = sb("ident", [P, P])
        ones = sb("ones", [P, P])
        gx = sb("gx", [P, C, N])
        gh = sb("gh", [P, C, N])
        gr = sb("gr", [P, C, N])
        stats = sb("stats", [P, C, 2, 6])
        mv = sb("mv", [P, C, 2])
        var_eps = sb("var_eps", [P, C])
        std = sb("std", [P, C])
        rstd = sb("rstd", [P, C])
        newt = sb("newt", [P, C])
        fv_row = sb("fv_row", [P, N])
        fv_col = sb("fv_col", [P, T])
        sim = sb("sim", [P, N + TOP])
        sim_rest = sb("sim_rest", [P, N + TOP])
        top1 = sb("top1", [P, TOP])
        drop1 = sb("drop1", [P, TOP])
        top8 = sb("top8", [P, TOP])
        marked = sb("marked", [P, N])
        pick = sb("pick", [P, T, N])
        adj = sb("adj", [P, T, N])
        dinv = sb("dinv", [P, N])
        hw_t = sb("hw_t", [P, T, S])

        loaded_consts = sem("loaded_consts")
        ones_ready = sem("ones_ready")
        x_loaded = sem("x_loaded")
        var_ready = sem("var_ready")
        std_ready = sem("std_ready")
        vec_steps = sem("vec_steps")
        h_ready = sem("h_ready")
        fv_ready = sem("fv_ready")
        pick_ready = sem("pick_ready")
        turned = sem("turned")
        adj_rows = sem("adj_rows")
        deg_ready = sem("deg_ready")
        mix_ready = sem("mix_ready")
        hw_ready = sem("hw_ready")
        hw_copied = sem("hw_copied")
        mixed = sem("mixed")
        relu_ready = sem("relu_ready")
        out_ready = sem("out_ready")
        stored = sem("stored")
        fence = sem("fence")
        sp_fence = sem("sp_fence")

        K_VEC = 15 + 5 * T + 2

        block = ctx.enter_context(nc.Block())

        @block.sync
        def _(sp):
            sp.dma_start(w_t[:], wT.rearrange("(c p) n -> p c n", p=P)).then_inc(loaded_consts, 16)
            sp.dma_start(bias1[:], b1).then_inc(loaded_consts, 16)
            sp.dma_start(bias2[:], b2).then_inc(loaded_consts, 16)
            sp.dma_start(ident[:], ident_in).then_inc(loaded_consts, 16)
            with sp.Fori(0, B) as b:
                sp.dma_start(gx[:], x[bass.ds(b, 1)].rearrange("b (c p) n -> p (b c) n", p=P)).then_inc(x_loaded, 16)
                sp.wait_ge(out_ready, b + 1)
                sp.dma_start(out[bass.ds(b, 1)].rearrange("b (c p) n -> p (b c) n", p=P), gx[:]).then_inc(stored, 16)
                sp.wait_ge(stored, 16 * b + 16)
                sp.sem_inc(sp_fence, 1)


        @block.scalar
        def _(act):
            with act.Fori(0, B) as b:
                act.wait_ge(var_ready, b + 1)
                nc.scalar.activation(std[:], var_eps[:], ACT.Sqrt).then_inc(std_ready, 1)

        @block.vector
        def _(dve):
            count = [0]

            nc.vector.memset(ones[:], 1.0).then_inc(ones_ready, 1)
            nc.vector.memset(sim[:, N:], -2.0).then_inc(ones_ready, 1)
            nc.vector.memset(drop1[:], -2.0).then_inc(ones_ready, 1)
            dve.wait_ge(ones_ready, 3)
            dve.wait_ge(loaded_consts, 64)
            with dve.Fori(0, B) as b:
                base = b * K_VEC

                def step(ins, held=False):
                    count[0] += 1
                    ins.then_inc(vec_steps, 1)
                    dve.wait_ge(vec_steps, base + count[0])
                    if held:
                        dve.sem_inc(fence, 1)

                dve.wait_ge(x_loaded, 16 * b + 16)
                for c in range(C):
                    for j in range(2):
                        step(nc.vector.bn_stats(stats[:, c, j, :], gx[:, c, j * HALF:(j + 1) * HALF]), held=True)
                for c in range(C):
                    step(nc.vector.bn_aggr(mv[:, c, :], stats[:, c, :, :]), held=True)
                nc.vector.tensor_scalar(var_eps[:], mv[:, :, 1], EPS, None, ALU.add).then_inc(var_ready, 1)
                dve.wait_ge(std_ready, b + 1)
                step(nc.vector.reciprocal(rstd[:], std[:]))
                step(nc.vector.tensor_tensor(newt[:], rstd[:], rstd[:], ALU.mult))
                step(nc.vector.tensor_tensor(newt[:], newt[:], var_eps[:], ALU.mult))
                step(nc.vector.tensor_scalar(newt[:], newt[:], -0.5, 1.5, ALU.mult, ALU.add))
                step(nc.vector.tensor_tensor(rstd[:], rstd[:], newt[:], ALU.mult))
                for c in range(C):
                    step(nc.vector.tensor_scalar(gh[:, c, :], gx[:, c, :], mv[:, c, 0:1], rstd[:, c:c + 1],
                                                 ALU.subtract, ALU.mult))
                nc.vector.tensor_scalar(gh[:], gh[:], 0.0, None, ALU.max).then_inc(h_ready, 1)
                dve.wait_ge(fv_ready, b + 1)
                step(nc.vector.tensor_copy(fv_row[:], ps_a[:, 0:N]))
                step(nc.vector.tensor_copy(fv_col[:], ps_b[:, 0:T]))
                for t in range(T):
                    step(nc.vector.tensor_scalar(sim[:, 0:N], fv_row[:], fv_col[:, t:t + 1], None, ALU.mult), held=True)
                    step(nc.vector.max(top1[:], sim[:, 0:N]), held=True)
                    step(nc.vector.tensor_copy(drop1[:, 0:1], top1[:, 0:1]), held=True)
                    step(nc.vector.match_replace(out=sim_rest[:], in_to_replace=drop1[:], in_values=sim[:], imm_value=-3.0), held=True)
                    step(nc.vector.max(top8[:], sim_rest[:, 0:N]), held=True)
                    nc.vector.match_replace(out=marked[:], in_to_replace=top8[:], in_values=sim_rest[:, 0:N],
                                            imm_value=1e30).then_inc(pick_ready, 1)
                    dve.wait_ge(pick_ready, b * 2 * T + 2 * t + 1)
                    nc.vector.tensor_scalar(pick[:, t, :], marked[:], 1e30, None, ALU.is_ge).then_inc(pick_ready, 1)
                dve.wait_ge(pick_ready, b * 2 * T + 2 * T)
                for u in range(T):
                    dve.wait_ge(turned, b * T + u + 1)
                    nc.vector.tensor_tensor(adj[:, u, :], pick[:, u, :], ps_a[:, 0:N], ALU.max).then_inc(adj_rows, 1)
                    dve.wait_ge(adj_rows, b * 2 * T + 2 * u + 1)
                    blk = adj[:, u, u * P:(u + 1) * P]
                    nc.vector.tensor_tensor(blk, blk, ident[:], ALU.max).then_inc(adj_rows, 1)
                dve.wait_ge(deg_ready, b + 1)
                step(nc.vector.reciprocal(dinv[:], ps_b[:, 0:N]))
                for t in range(T):
                    nc.vector.tensor_tensor(adj[:, t, :], adj[:, t, :], dinv[:], ALU.mult).then_inc(mix_ready, 1)
                for layer in range(2):
                    dve.wait_ge(hw_ready, 2 * b + layer + 1)
                    nc.vector.tensor_copy(hw_t[:].rearrange("p t s -> p (t s)"), ps_a[:]).then_inc(hw_copied, 1)
                    dve.wait_ge(mixed, 2 * b + layer + 1)
                    for c in range(C):
                        src = ps_b[:, c * N:(c + 1) * N]
                        if layer == 0:
                            nc.vector.tensor_scalar(gr[:, c, :], src, bias1[:, c:c + 1], 0.0,
                                                    ALU.add, ALU.max).then_inc(relu_ready, 1)
                        elif c < C - 1:
                            step(nc.vector.scalar_tensor_tensor(out=gx[:, c, :], in0=src, scalar=bias2[:, c:c + 1],
                                                                in1=gx[:, c, :], op0=ALU.add, op1=ALU.add))
                        else:
                            nc.vector.scalar_tensor_tensor(out=gx[:, c, :], in0=src, scalar=bias2[:, c:c + 1],
                                                           in1=gx[:, c, :], op0=ALU.add, op1=ALU.add
                                                           ).then_inc(out_ready, 1)
            assert count[0] == K_VEC

        @block.tensor
        def _(pe):
            pe.wait_ge(loaded_consts, 64)
            pe.wait_ge(ones_ready, 1)
            with pe.Fori(0, B) as b:
                pe.wait_ge(h_ready, b + 1)
                for nh in range(NH):
                    for c in range(C):
                        nc.tensor.matmul(ps_a[:, nh * HALF:(nh + 1) * HALF], ones[:],
                                         gh[:, c, nh * HALF:(nh + 1) * HALF], start=(c == 0), stop=(c == C - 1))
                for t in range(T):
                    for c in range(C):
                        last = nc.tensor.matmul(ps_b[:, t:t + 1], gh[:, c, t * P:(t + 1) * P], ones[:, 0:1],
                                                start=(c == 0), stop=(c == C - 1))
                last.then_inc(fv_ready, 1)
                pe.wait_ge(pick_ready, b * 2 * T + 2 * T)
                for u in range(T):
                    if u > 0:
                        pe.wait_ge(adj_rows, b * 2 * T + 2 * u)
                    for t in range(T):
                        last = nc.tensor.transpose(ps_a[:, t * P:(t + 1) * P], pick[:, t, u * P:(u + 1) * P], ident[:])
                    last.then_inc(turned, 1)
                pe.wait_ge(adj_rows, b * 2 * T + 2 * T)
                for nh in range(NH):
                    for t in range(T):
                        last = nc.tensor.matmul(ps_b[:, nh * HALF:(nh + 1) * HALF], ones[:],
                                                adj[:, t, nh * HALF:(nh + 1) * HALF], start=(t == 0), stop=(t == T - 1))
                last.then_inc(deg_ready, 1)
                pe.wait_ge(mix_ready, b * T + T)
                for layer, src in ((0, gh), (1, gr)):
                    if layer == 1:
                        pe.wait_ge(relu_ready, 2 * b + 2)
                    for t in range(T):
                        for c in range(C):
                            last = nc.tensor.matmul(ps_a[:, t * S:(t + 1) * S], src[:, c, t * P:(t + 1) * P],
                                                    w_t[:, c, :], start=(c == 0), stop=(c == C - 1))
                    last.then_inc(hw_ready, 1)
                    pe.wait_ge(hw_copied, 2 * b + layer + 1)
                    for m in range(C):
                        for nh in range(NH):
                            for t in range(T):
                                last = nc.tensor.matmul(
                                    ps_b[:, m * N + nh * HALF:m * N + (nh + 1) * HALF],
                                    hw_t[:, t, m * P:(m + 1) * P], adj[:, t, nh * HALF:(nh + 1) * HALF],
                                    start=(t == 0), stop=(t == T - 1))
                    last.then_inc(mixed, 1)


def kernel(x, adj, L0_gnn_b1, L0_gnn_b2):
    import numpy as np
    import concourse.bacc as bacc
    from concourse.bass_utils import run_bass_kernel_spmd as run

    nc = bacc.Bacc("TRN2", target_bir_lowering=False, num_devices=1)
    arrays = {
        "x_in": np.ascontiguousarray(x),
        "w_t_in": np.ascontiguousarray(np.asarray(adj).T),
        "b1_in": np.ascontiguousarray(np.asarray(L0_gnn_b1).reshape(-1, P).T),
        "b2_in": np.ascontiguousarray(np.asarray(L0_gnn_b2).reshape(-1, P).T),
        "ident_in": np.eye(P, dtype=np.float32),
    }
    args = [nc.dram_tensor(k, a.shape, mybir.dt.from_np(a.dtype), kind="ExternalInput").ap() for k, a in arrays.items()]
    out = nc.dram_tensor("out", arrays["x_in"].shape, F32, kind="ExternalOutput").ap()
    gnn_kernel(nc, *args, out)
    r = run(nc, [arrays], core_ids=[0])
    return r.results[0]["out"]
```

```python
from contextlib import ExitStack

import concourse.bass as bass
from concourse import mybir

ALU = mybir.AluOpType
ACT = mybir.ActivationFunctionType
AX = mybir.AxisListType
F32 = mybir.dt.float32
F32R = mybir.dt.float32r
U32 = mybir.dt.uint32

P = 128
TOP = 8
EPS = 1e-5
HALF = 512
XS = 8
HS = 4


class Step:

    def __init__(self, k, turn=0):
        self.k, self.turn = k, turn

    def has(self, off, batches):
        return not isinstance(self.turn, int) or 0 <= self.k + off < batches

    def val(self, per=1, off=0, plus=0):
        fixed = per * (self.k + off) + plus
        return fixed if isinstance(self.turn, int) else self.turn * (8 * per) + fixed

    def pair(self, off, per=1, plus=0):
        fixed = per * ((self.k + off) // 2) + plus
        return fixed if isinstance(self.turn, int) else self.turn * (4 * per) + fixed

    def round(self, off, plus=0):
        fixed = 16 * ((self.k + off) // XS) + plus
        return fixed if isinstance(self.turn, int) else self.turn * 16 + fixed


def gnn_kernel(nc, x, wT, b1, b2, ident_in, out):
    B, S, N = x.shape
    C = S // P
    T = N // P
    NH = N // HALF
    U = C * NH
    DEG = TOP + 1
    COLS = TOP + 2
    GEN_VEC = 11 + 5 * T

    LEAD, LOOP0, TURNS = 5, 2, (B - 8) // 8
    assert LOOP0 + 8 * TURNS - 1 + LEAD < B and B % 8 == 0

    def run_steps(eng, step):
        for k in range(-LEAD, LOOP0):
            step(Step(k))
        with eng.Fori(0, TURNS) as turn:
            for k in range(LOOP0, LOOP0 + 8):
                step(Step(k, turn))
        for k in range(LOOP0 + 8 * TURNS, B + 2):
            step(Step(k))

    with ExitStack() as ctx:
        def sb(name, shape, dt=F32):
            return ctx.enter_context(nc.sbuf_tensor(name, shape, dt))

        def sem(name):
            return ctx.enter_context(nc.semaphore(name))

        def psum(name, cols):
            return ctx.enter_context(nc.psum_tensor(name, [P, cols], F32))

        ps_main = psum("ps_main", U * HALF)
        ps_fv = psum("ps_fv", N)
        ps_top = psum("ps_top", HALF)
        ps_c2 = psum("ps_c2", HALF)

        w_t = sb("w_t", [P, C, S])
        w_hi = sb("w_hi", [P, C, S], F32R)
        w_lo = sb("w_lo", [P, C, S], F32R)
        bias1 = sb("bias1", [P, C])
        bias2 = sb("bias2", [P, C])
        b1_ninth = sb("b1_ninth", [P, C, 2])
        b1_8ninth = sb("b1_8ninth", [P, C, 2])
        b2_pair = sb("b2_pair", [P, C, 2])
        ident = sb("ident", [P, P])
        ones = sb("ones", [P, P])
        pick_f = sb("pick_f", [P, 2, P])
        pick_row = sb("pick_row", [P, 2, P], F32R)
        minus_half = sb("minus_half", [P, 2, C])
        x_sb = sb("x_sb", [P, XS, C, N])
        work = sb("work", [P, 4, C, N])
        h_f, r_f = work[:, 0:2], work[:, 2:4]
        h_hi = sb("h_hi", [P, HS, C, N], F32R)
        h_lo = sb("h_lo", [P, HS, C, N], F32R)
        r_hi = sb("r_hi", [P, C, N], F32R)
        r_lo = sb("r_lo", [P, C, N], F32R)
        stats = sb("stats", [P, 2, C, NH, 6])
        mv = sb("mv", [P, 4, C, 2])
        var_eps = sb("var_eps", [P, 2, C])
        rstd = sb("rstd", [P, 2, 2, C])
        mr = sb("mr", [P, 2, 2, C])
        neg_mr = sb("neg_mr", [P, 2, 2, C])
        top_h = sb("top_h", [P, HS, C, COLS])
        relu_bias = sb("relu_bias", [P, 2, C, 2])
        r8_raw = sb("r8_raw", [P, 2, C, 2])
        r8 = sb("r8", [P, 2, C, 2])
        r8_rest = sb("r8_rest", [P, 2, C, 2])
        out_bias = sb("out_bias", [P, 2, C, 2])
        relu_top = sb("relu_top", [P, C, TOP])
        top_sum = sb("top_sum", [P, 2, C])
        r_sum = sb("r_sum", [P, 2, C, NH])
        r_all = sb("r_all", [P, C])
        r_rest = sb("r_rest", [P, C])
        rho = sb("rho", [P, 2, C])
        sim = sb("sim", [P, N + TOP])
        sim_rest = sb("sim_rest", [P, N + TOP])
        row_a = sb("row_a", [P, N])
        top1 = sb("top1", [P, TOP])
        drop1 = sb("drop1", [P, TOP])
        top8 = sb("top8", [P, TOP])
        found = sb("found", [P, TOP], U32)
        idx = sb("idx", [P, 2, TOP], U32)
        signs = sb("signs", [P, 2])
        flags = sb("flags", [P, B // 2])
        least_signs = sb("least_signs", [P, 1])
        least = sb("least", [P, 1], U32)
        fv_col = sb("fv_col", [P, T])

        consts_loaded = sem("consts_loaded")
        memsets_done = sem("memsets_done")
        consts_done = sem("consts_done")
        x_loaded = [sem(f"x_loaded{i}") for i in range(XS)]
        x_stored = [sem(f"x_stored{i}") for i in range(XS)]

        def last_extra(i):
            return 16 * (C - 1) if i == XS - 1 else 0

        names = """bn_done aggr_done coef_steps coef_ready h_made h_hi_ready h_lo_vec h_lo_pool fv_ready fv_copied signed
        top_steps idx_ready gathered top_summed top_ready bias_ready r8_steps r8_ready rest_ready c2_ready out_bias_ready
        top_relued m1_done r_made fix_steps rho_ready scattered r_hi_ready r_lo_ready m2_done out_done
        flags_ready least_steps least_ready vec_fence pool_fence sp_fence
        g_x g_var g_std g_vec g_h g_fv g_pick g_turned g_rows g_deg g_mix g_hw g_hwc g_mixed g_relu g_result g_out
        g_stored""".split()
        q = {n: sem(n) for n in names}

        x_dram = x.rearrange("b (c p) n -> b p c n", p=P)
        out_dram = out.rearrange("b (c p) n -> b p c n", p=P)

        block = ctx.enter_context(nc.Block())

        gx, gh, gr = x_sb[:, 0], x_sb[:, 1], x_sb[:, 2]
        hw_t = x_sb[:, 3].rearrange("p c n -> p (c n)").rearrange("p (t s) -> p t s", t=T)
        pick = x_sb[:, XS - 4:XS].rearrange("p a c n -> p (a c) n")
        mix = work[:].rearrange("p a c n -> p (a c) n")
        marked = work[:, 0, 0]
        half_banks = [ps_fv[:, 0:HALF], ps_fv[:, HALF:2 * HALF], ps_top[:], ps_c2[:]]

        def load_least(eng):
            eng.wait_ge(q["least_ready"], 1)
            one = eng.value_load(least[0:1, 0:1], min_val=0, max_val=1)
            two = eng.value_load(least[1:2, 0:1], min_val=0, max_val=1)
            general = eng.alloc_register("general")
            eng.reg_mov(general, one + two)
            return general

        def general_sync(sp):
            for i in range(XS):
                sp.wait_ge(x_stored[i], 16 * (B // XS) + last_extra(i))
            with sp.If_ne(load_least(sp), 0):
                with sp.Fori(0, B) as b:
                    sp.dma_start(gx, x_dram[bass.ds(b, 1)].rearrange("b p c n -> p (b c) n")).then_inc(q["g_x"], 16)
                    sp.wait_ge(q["g_out"], b + 1)
                    sp.dma_start(out_dram[bass.ds(b, 1)].rearrange("b p c n -> p (b c) n"), gx
                                 ).then_inc(q["g_stored"], 16)
                    sp.wait_ge(q["g_stored"], 16 * b + 16)
                    sp.sem_inc(q["sp_fence"], 1)

        def general_pool(pool):
            with pool.If_ne(load_least(pool), 0):
                with pool.Fori(0, B) as b:
                    pool.wait_ge(q["g_var"], b + 1)
                    pool.sem_inc(q["pool_fence"], 1)
                    nc.gpsimd.tensor_tensor(rstd[:, 0, 0], var_eps[:, 0], minus_half[:, 0], ALU.pow
                                            ).then_inc(q["g_std"], 1)

        def general_vector(dve):
            with dve.If_ne(load_least(dve), 0):
                with dve.Fori(0, B) as b:
                    base = b * GEN_VEC
                    count = [0]

                    def step(ins):
                        count[0] += 1
                        ins.then_inc(q["g_vec"], 1)
                        dve.wait_ge(q["g_vec"], base + count[0])
                        dve.sem_inc(q["vec_fence"], 1)

                    dve.wait_ge(q["g_x"], 16 * b + 16)
                    for c in range(C):
                        for j in range(NH):
                            step(nc.vector.bn_stats(stats[:, 0, c, j, :], gx[:, c, j * HALF:(j + 1) * HALF]))
                    for c in range(C):
                        step(nc.vector.bn_aggr(mv[:, 0, c, :], stats[:, 0, c, :, :]))
                    nc.vector.tensor_scalar(var_eps[:, 0], mv[:, 0, :, 1], EPS, None, ALU.add
                                            ).then_inc(q["g_var"], 1)
                    dve.wait_ge(q["g_std"], b + 1)
                    for c in range(C):
                        step(nc.vector.tensor_scalar(gh[:, c, :], gx[:, c, :], mv[:, 0, c, 0:1],
                                                     rstd[:, 0, 0, c:c + 1], ALU.subtract, ALU.mult))
                    nc.vector.tensor_scalar(gh, gh, 0.0, None, ALU.max).then_inc(q["g_h"], 1)
                    dve.wait_ge(q["g_fv"], b + 1)
                    step(nc.vector.tensor_copy(row_a[:], ps_main[:, 0:N]))
                    step(nc.vector.tensor_copy(fv_col[:], ps_top[:, 0:T]))
                    for t in range(T):
                        step(nc.vector.tensor_scalar(sim[:, 0:N], row_a[:], fv_col[:, t:t + 1], None, ALU.mult))
                        step(nc.vector.max(top1[:], sim[:, 0:N]))
                        step(nc.vector.tensor_copy(drop1[:, 0:1], top1[:, 0:1]))
                        step(nc.vector.match_replace(out=sim_rest[:], in_to_replace=drop1[:], in_values=sim[:],
                                                     imm_value=-3.0))
                        step(nc.vector.max(top8[:], sim_rest[:, 0:N]))
                        nc.vector.match_replace(out=marked, in_to_replace=top8[:], in_values=sim_rest[:, 0:N],
                                                imm_value=1e30).then_inc(q["g_pick"], 1)
                        dve.wait_ge(q["g_pick"], b * 2 * T + 2 * t + 1)
                        nc.vector.tensor_scalar(pick[:, t, :], marked, 1e30, None, ALU.is_ge
                                                ).then_inc(q["g_pick"], 1)
                    dve.wait_ge(q["g_pick"], b * 2 * T + 2 * T)
                    for u in range(T):
                        dve.wait_ge(q["g_turned"], b * T + u + 1)
                        nc.vector.tensor_tensor(mix[:, u, :], pick[:, u, :], ps_main[:, 0:N], ALU.max
                                                ).then_inc(q["g_rows"], 1)
                        dve.wait_ge(q["g_rows"], b * 2 * T + 2 * u + 1)
                        diagonal = mix[:, u, u * P:(u + 1) * P]
                        nc.vector.tensor_tensor(diagonal, diagonal, ident[:], ALU.max).then_inc(q["g_rows"], 1)
                    dve.wait_ge(q["g_deg"], b + 1)
                    step(nc.vector.reciprocal(row_a[:], ps_fv[:, 0:N]))
                    for t in range(T):
                        nc.vector.tensor_tensor(mix[:, t, :], mix[:, t, :], row_a[:], ALU.mult
                                                ).then_inc(q["g_mix"], 1)
                    for layer in range(2):
                        dve.wait_ge(q["g_hw"], 2 * b + layer + 1)
                        nc.vector.tensor_copy(hw_t.rearrange("p t s -> p (t s)"), ps_main[:]).then_inc(q["g_hwc"], 1)
                        dve.wait_ge(q["g_mixed"], 2 * b + layer + 1)
                        for u in range(U):
                            c, at = u // NH, slice(u % NH * HALF, (u % NH + 1) * HALF)
                            if layer == 0:
                                nc.vector.tensor_scalar(gr[:, c, at], half_banks[u], bias1[:, c:c + 1], 0.0,
                                                        ALU.add, ALU.max).then_inc(q["g_relu"], 1)
                            else:
                                nc.vector.scalar_tensor_tensor(
                                    out=gx[:, c, at], in0=half_banks[u], scalar=bias2[:, c:c + 1], in1=gx[:, c, at],
                                    op0=ALU.add, op1=ALU.add).then_inc(q["g_result"], 1)
                    dve.wait_ge(q["g_result"], b * U + U)
                    dve.sem_inc(q["g_out"], 1)
                    assert count[0] == GEN_VEC

        def general_tensor(pe):
            with pe.If_ne(load_least(pe), 0):
                with pe.Fori(0, B) as b:
                    pe.wait_ge(q["g_h"], b + 1)
                    for nh in range(NH):
                        for c in range(C):
                            nc.tensor.matmul(ps_main[:, nh * HALF:(nh + 1) * HALF], ones[:],
                                             gh[:, c, nh * HALF:(nh + 1) * HALF], start=(c == 0), stop=(c == C - 1))
                    for t in range(T):
                        for c in range(C):
                            last = nc.tensor.matmul(ps_top[:, t:t + 1], gh[:, c, t * P:(t + 1) * P], ones[:, 0:1],
                                                    start=(c == 0), stop=(c == C - 1))
                    last.then_inc(q["g_fv"], 1)
                    pe.wait_ge(q["g_pick"], b * 2 * T + 2 * T)
                    for u in range(T):
                        if u > 0:
                            pe.wait_ge(q["g_rows"], b * 2 * T + 2 * u)
                        for t in range(T):
                            last = nc.tensor.transpose(ps_main[:, t * P:(t + 1) * P],
                                                       pick[:, t, u * P:(u + 1) * P], ident[:])
                        last.then_inc(q["g_turned"], 1)
                    pe.wait_ge(q["g_rows"], b * 2 * T + 2 * T)
                    for nh in range(NH):
                        for t in range(T):
                            last = nc.tensor.matmul(ps_fv[:, nh * HALF:(nh + 1) * HALF], ones[:],
                                                    mix[:, t, nh * HALF:(nh + 1) * HALF],
                                                    start=(t == 0), stop=(t == T - 1))
                    last.then_inc(q["g_deg"], 1)
                    pe.wait_ge(q["g_mix"], b * T + T)
                    for layer, y in ((0, gh), (1, gr)):
                        if layer == 1:
                            pe.wait_ge(q["g_relu"], U * b + U)
                        for t in range(T):
                            for c in range(C):
                                last = nc.tensor.matmul(ps_main[:, t * S:(t + 1) * S], y[:, c, t * P:(t + 1) * P],
                                                        w_t[:, c, :], start=(c == 0), stop=(c == C - 1))
                        last.then_inc(q["g_hw"], 1)
                        pe.wait_ge(q["g_hwc"], 2 * b + layer + 1)
                        for u in range(U):
                            m, nh = u // NH, u % NH
                            for t in range(T):
                                last = nc.tensor.matmul(half_banks[u], hw_t[:, t, m * P:(m + 1) * P],
                                                        mix[:, t, nh * HALF:(nh + 1) * HALF],
                                                        start=(t == 0), stop=(t == T - 1))
                        last.then_inc(q["g_mixed"], 1)

        @block.sync
        def _(sp):
            for i in range(2):
                sp.dma_start(x_sb[:, i], x_dram[i]).then_inc(x_loaded[i], 16)
            sp.dma_start(w_t[:], wT.rearrange("(c p) n -> p c n", p=P)).then_inc(consts_loaded, 16)
            sp.dma_start(bias1[:], b1).then_inc(consts_loaded, 16)
            sp.dma_start(bias2[:], b2).then_inc(consts_loaded, 16)
            sp.dma_start(ident[:], ident_in).then_inc(consts_loaded, 16)
            for i in range(2, XS):
                sp.dma_start(x_sb[:, i], x_dram[i]).then_inc(x_loaded[i], 16)
            with sp.Fori(1, B // XS) as turn:
                for i in range(XS):
                    sp.wait_ge(x_stored[i], turn * 16)
                    sp.dma_start(x_sb[:, i], x_dram[bass.ds(turn * XS + i, 1)].rearrange("b p c n -> p (b c) n")
                                 ).then_inc(x_loaded[i], 16)
            general_sync(sp)

        @block.scalar
        def _(act):
            def step(s):
                odd = s.k % 2 == 1
                if odd and s.has(1, B):
                    g1 = (s.k + 1) // 2 % 2
                    act.wait_ge(q["fv_ready"], s.pair(1, plus=1))
                    nc.scalar.activation(sim[0:2, 0:N], ps_fv[0:2, :], ACT.Copy).then_inc(q["fv_copied"], 1)
                if s.has(3, B):
                    bb = s.k + 3
                    act.wait_ge(q["coef_ready"], s.pair(2 if s.k % 2 == 0 else 3, plus=1))
                    if not isinstance(s.turn, int) or bb >= 2:
                        if odd:
                            act.wait_ge(q["h_lo_vec"], s.pair(3, 2, -1))
                            act.wait_ge(q["h_lo_pool"], s.pair(3, 2, -1))
                        else:
                            act.wait_ge(q["h_lo_vec"], s.pair(2, 2))
                            act.wait_ge(q["h_lo_pool"], s.pair(2, 2))
                    norm_h(s, 0)
                    if s.k <= 0:
                        high_h(s, 0)
                        norm_h(s, 1)
                        high_h(s, 1)
                if s.has(0, B):
                    g, e, slot = s.k // 2 % 2, s.k % 2, s.k % 2
                    act.wait_ge(q["bias_ready"], s.pair(-1 if odd else 0, plus=1))
                    for m in range(C):
                        nc.scalar.activation(relu_top[:, m], ps_top[:, (2 * m + e) * COLS:(2 * m + e) * COLS + TOP],
                                             ACT.Relu, bias=relu_bias[:, g, m, e:e + 1], scale=1.0 / DEG ** 2,
                                             accum_out=top_sum[:, slot, m:m + 1]).then_inc(q["top_relued"], 1)
                    relu_half(s, 0)
                if s.has(3, B) and s.k > 0:
                    norm_h(s, 1)
                    high_h(s, 0)
                if s.has(0, B):
                    relu_half(s, 1)
                if odd and s.has(1, B):
                    act.wait_ge(q["fv_copied"], s.pair(1, plus=1))
                    nc.scalar.activation(row_a[0:2, :], sim[0:2, 0:N], ACT.Sign,
                                         accum_out=signs[0:2, g1:g1 + 1]).then_inc(q["signed"], 1)
                if s.has(-2, B):
                    i = (s.k - 2) % XS
                    if s.k - 2 < B - 1:
                        act.wait_ge(q["out_done"], s.val(U, -2, U))
                        act.dma_start(out_at(s, -2), x_sb[:, i]).then_inc(x_stored[i], 16)
                    else:
                        for m in range(C):
                            act.wait_ge(q["out_done"], s.val(U, -2, (m + 1) * NH))
                            act.dma_start(out_at(s, -2)[:, m], x_sb[:, i, m]).then_inc(x_stored[i], 16)
                if s.has(3, B) and s.k > 0:
                    high_h(s, 1)
                if s.has(0, B):
                    act.wait_ge(q["scattered"], s.val(1, 0, 1))
                    if not isinstance(s.turn, int) or s.k >= 1:
                        act.wait_ge(q["m2_done"], s.val(U))
                    for c in range(C):
                        nc.scalar.activation(r_hi[:, c], r_f[:, s.k % 2, c], ACT.Copy).then_inc(q["r_hi_ready"], 1)

            def relu_half(s, m):
                g, e = s.k // 2 % 2, s.k % 2
                for nh in range(NH):
                    u = m * NH + nh
                    act.wait_ge(q["m1_done"], s.val(U, 0, u + 1))
                    nc.scalar.activation(r_f[:, e, m, nh * HALF:(nh + 1) * HALF],
                                         ps_main[:, u * HALF:(u + 1) * HALF], ACT.Relu,
                                         bias=relu_bias[:, g, m, e:e + 1], scale=1.0 / DEG ** 2,
                                         accum_out=r_sum[:, e, m, nh:nh + 1]).then_inc(q["r_made"], 1)

            def norm_h(s, c):
                bb = s.k + 3
                nc.scalar.activation(h_f[:, bb % 2, c], x_sb[:, bb % XS, c], ACT.Relu,
                                     bias=neg_mr[:, bb // 2 % 2, bb % 2, c:c + 1],
                                     scale=rstd[:, bb // 2 % 2, bb % 2, c:c + 1],
                                     accum_out=top_h[:, bb % HS, c, COLS - 1:COLS]).then_inc(q["h_made"], 1)

            def high_h(s, c):
                bb = s.k + 3
                act.wait_ge(q["h_made"], s.val(C, 3, c + 1))
                nc.scalar.activation(h_hi[:, bb % HS, c], h_f[:, bb % 2, c], ACT.Copy).then_inc(q["h_hi_ready"], 1)

            def out_at(s, off):
                if isinstance(s.turn, int):
                    return out_dram[s.k + off]
                return out_dram[bass.ds(s.val(1, off), 1)].rearrange("b p c n -> p (b c) n")

            run_steps(act, step)
            for i in range(XS):
                act.wait_ge(x_stored[i], 16 * (B // XS) + last_extra(i))

        @block.gpsimd
        def _(pool):
            def hold(s, name, value):
                pool.wait_ge(q[name], value)
                pool.sem_inc(q["pool_fence"], 1)

            def load_idx(e, g):
                return nc.values_load_multi_w_load_instructions(
                    idx[e:e + 1, g, :], engines=[mybir.EngineType.Pool], min_val=0, max_val=N - 1,
                    skip_runtime_bounds_check_because="idx is clamped to N - 1 and unsigned")[1]

            nc.gpsimd.memset(minus_half[:], -0.5).then_inc(q["pool_fence"], 1)
            pool.wait_ge(q["pool_fence"], 1)

            def low_h(s, c):
                bb = s.k + 3
                pool.wait_ge(q["h_hi_ready"], s.val(C, 3, c + 1))
                nc.gpsimd.tensor_tensor(h_lo[:, bb % HS, c], h_f[:, bb % 2, c], h_hi[:, bb % HS, c].bitcast(F32),
                                        ALU.subtract).then_inc(q["h_lo_pool"], 1)

            def coefficients(s):
                j = (s.k + 4) // 2 % 2
                mv_pair = mv[:, (s.k + 4) % 4:(s.k + 4) % 4 + 2]
                hold(s, "aggr_done", s.pair(4, 2 * C, 2 * C))
                nc.gpsimd.tensor_scalar(var_eps[:], mv_pair[:, :, :, 1], EPS, None, ALU.add
                                        ).then_inc(q["coef_steps"], 1)
                hold(s, "coef_steps", s.pair(4, 3, 1))
                nc.gpsimd.tensor_tensor(rstd[:, j], var_eps[:], minus_half[:], ALU.pow
                                        ).then_inc(q["coef_steps"], 1)
                hold(s, "coef_steps", s.pair(4, 3, 2))
                nc.gpsimd.tensor_tensor(mr[:, j], mv_pair[:, :, :, 0], rstd[:, j], ALU.mult
                                        ).then_inc(q["coef_steps"], 1)
                hold(s, "coef_steps", s.pair(4, 3, 3))
                nc.gpsimd.tensor_scalar(neg_mr[:, j], mr[:, j], -1.0, None, ALU.mult
                                        ).then_inc(q["coef_ready"], 1)

            def gather(s):
                g = (s.k + 1) // 2 % 2
                hold(s, "idx_ready", s.pair(1, plus=1))
                for e in range(2):
                    sl = (s.k + 1 + e) % HS
                    for t, v in enumerate(load_idx(e, g)):
                        last = nc.gpsimd.tensor_tensor(
                            top_h[:, sl, :, t:t + 1], h_hi[:, sl, :, bass.ds(v, 1)].bitcast(F32),
                            h_lo[:, sl, :, bass.ds(v, 1)].bitcast(F32), ALU.add)
                last.then_inc(q["gathered"], 1)

            def scatter(s):
                nodes = load_idx(s.k % 2, s.k // 2 % 2)
                hold(s, "rho_ready", s.val(1, 0, 1))
                for v in nodes:
                    last = nc.gpsimd.tensor_copy(r_f[:, s.k % 2, :, bass.ds(v, 1)],
                                                 rho[:, s.k % 2, :].rearrange("p (c o) -> p c o", o=1))
                last.then_inc(q["scattered"], 1)

            def keep_flag(s):
                g = (s.k + 1) // 2 % 2
                hold(s, "signed", s.pair(1, plus=1))
                at = s.pair(1)
                spot = flags[0:2, at:at + 1] if isinstance(s.turn, int) else flags[0:2, bass.ds(at, 1)]
                nc.gpsimd.tensor_copy(spot, signs[0:2, g:g + 1]).then_inc(q["flags_ready"], 1)

            def step(s):
                if s.k % 2 == 0:
                    if s.has(3, B):
                        low_h(s, 0)
                    if s.has(0, B):
                        scatter(s)
                    if s.has(4, B):
                        coefficients(s)
                else:
                    if s.has(1, B):
                        gather(s)
                    if s.has(0, B):
                        scatter(s)
                    if s.has(3, B):
                        low_h(s, 1)
                    if s.has(1, B):
                        keep_flag(s)

            run_steps(pool, step)
            general_pool(pool)

        @block.vector
        def _(dve):
            def hold(name, value):
                dve.wait_ge(q[name], value)
                dve.sem_inc(q["vec_fence"], 1)

            def rows_top(s):
                g = (s.k + 1) // 2 % 2
                hold("fv_copied", s.pair(1, plus=1))
                nc.vector.max(top1[0:2], sim[0:2, 0:N]).then_inc(q["top_steps"], 1)
                hold("top_steps", s.pair(1, 5, 1))
                nc.vector.tensor_copy(drop1[0:2, 0:1], top1[0:2, 0:1]).then_inc(q["top_steps"], 1)
                hold("top_steps", s.pair(1, 5, 2))
                nc.vector.match_replace(out=sim_rest[0:2], in_to_replace=drop1[0:2], in_values=sim[0:2],
                                        imm_value=-3.0).then_inc(q["top_steps"], 1)
                hold("top_steps", s.pair(1, 5, 3))
                nc.vector.max(top8[0:2], sim_rest[0:2, 0:N]).then_inc(q["top_steps"], 1)
                hold("top_steps", s.pair(1, 5, 4))
                nc.vector.max_index(found[0:2], top8[0:2], sim_rest[0:2, 0:N]).then_inc(q["top_steps"], 1)
                hold("top_steps", s.pair(1, 5, 5))
                nc.vector.tensor_scalar(idx[0:2, g, :], found[0:2], N - 1, None, ALU.min).then_inc(q["idx_ready"], 1)

            def bn(s, off):
                i, e, m4 = (s.k + off) % XS, (s.k + off) % 2, (s.k + off) % 4
                dve.wait_ge(x_loaded[i], s.round(off, 16))
                for c in range(C):
                    for j in range(NH):
                        nc.vector.bn_stats(stats[:, e, c, j, :], x_sb[:, i, c, j * HALF:(j + 1) * HALF]
                                           ).then_inc(q["bn_done"], 1)
                hold("bn_done", s.val(C * NH, off, C * NH))
                for c in range(C):
                    nc.vector.bn_aggr(mv[:, m4, c, :], stats[:, e, c, :, :]).then_inc(q["aggr_done"], 1)

            def fix(s):
                e, g = s.k % 2, s.k // 2 % 2
                dve.wait_ge(q["r_made"], s.val(U, 0, U))
                nc.vector.tensor_tensor(r_all[:], r_sum[:, e, :, 0], r_sum[:, e, :, 1], ALU.add
                                        ).then_inc(q["fix_steps"], 1)
                dve.wait_ge(q["fix_steps"], s.val(2, 0, 1))
                nc.vector.tensor_tensor(r_rest[:], r_all[:], top_sum[:, e, :], ALU.subtract
                                        ).then_inc(q["fix_steps"], 1)
                dve.wait_ge(q["fix_steps"], s.val(2, 0, 2))
                dve.wait_ge(q["rest_ready"], s.pair(-1 if s.k % 2 else 0, plus=1))
                nc.vector.scalar_tensor_tensor(out=rho[:, e, :], in0=r_rest[:], scalar=DEG / N,
                                               in1=r8_rest[:, g, :, e], op0=ALU.mult, op1=ALU.add
                                               ).then_inc(q["rho_ready"], 1)

            def out_half(s, m):
                i, e, g = (s.k - 1) % XS, (s.k - 1) % 2, (s.k - 1) // 2 % 2
                for nh in range(NH):
                    u = m * NH + nh
                    part = x_sb[:, i, m, nh * HALF:(nh + 1) * HALF]
                    dve.wait_ge(q["m2_done"], s.val(U, -1, u + 1))
                    nc.vector.scalar_tensor_tensor(out=part, in0=ps_main[:, u * HALF:(u + 1) * HALF],
                                                   scalar=out_bias[:, g, m, e:e + 1], in1=part,
                                                   op0=ALU.add, op1=ALU.add).then_inc(q["out_done"], 1)

            def low_h(s, c):
                bb = s.k + 3
                dve.wait_ge(q["h_hi_ready"], s.val(C, 3, c + 1))
                nc.vector.tensor_tensor(h_lo[:, bb % HS, c], h_f[:, bb % 2, c], h_hi[:, bb % HS, c].bitcast(F32),
                                        ALU.subtract).then_inc(q["h_lo_vec"], 1)

            def low_r(s, c):
                dve.wait_ge(q["r_hi_ready"], s.val(C, 0, c + 1))
                nc.vector.tensor_tensor(r_lo[:, c], r_f[:, s.k % 2, c], r_hi[:, c].bitcast(F32),
                                        ALU.subtract).then_inc(q["r_lo_ready"], 1)

            def sum_top(s):
                sl = (s.k + 1) % HS
                dve.wait_ge(q["gathered"], s.pair(1, plus=1))
                nc.vector.tensor_reduce(top_h[:, sl:sl + 2, :, TOP], top_h[:, sl:sl + 2, :, 0:TOP], AX.X, ALU.add
                                        ).then_inc(q["top_summed"], 1)

            def small_vectors(s):
                g = (s.k + 1) // 2 % 2
                small = ps_top[:, 0:2 * C * COLS].rearrange("p (m e k) -> p m e k", m=C, e=2)
                dve.wait_ge(q["top_ready"], s.pair(1, plus=1))
                nc.vector.scalar_tensor_tensor(out=r8_raw[:, g], in0=small[:, :, :, TOP + 1], scalar=TOP / DEG / N,
                                               in1=b1_8ninth[:], op0=ALU.mult, op1=ALU.add).then_inc(q["r8_steps"], 1)
                nc.vector.scalar_tensor_tensor(out=relu_bias[:, g], in0=small[:, :, :, TOP], scalar=1.0 / DEG ** 2,
                                               in1=b1_ninth[:], op0=ALU.mult, op1=ALU.add
                                               ).then_inc(q["bias_ready"], 1)
                dve.wait_ge(q["r8_steps"], s.pair(1, 1, 1))
                nc.vector.tensor_scalar(r8[:, g], r8_raw[:, g], 0.0, None, ALU.max).then_inc(q["r8_ready"], 1)
                dve.wait_ge(q["r8_ready"], s.pair(1, plus=1))
                nc.vector.tensor_scalar(r8_rest[:, g], r8[:, g], DEG / N - 1.0, None, ALU.mult
                                        ).then_inc(q["rest_ready"], 1)

            def second_bias(s):
                g = s.k // 2 % 2
                dve.wait_ge(q["c2_ready"], s.pair(0, plus=1))
                nc.vector.tensor_tensor(out_bias[:, g], ps_c2[:, 0:2 * C].rearrange("p (m e) -> p m e", m=C),
                                        b2_pair[:], ALU.add).then_inc(q["out_bias_ready"], 1)

            nc.vector.memset(ones[:], 1.0).then_inc(memsets_done, 1)
            nc.vector.memset(sim[:, N:], -2.0).then_inc(memsets_done, 1)
            nc.vector.memset(drop1[:], -2.0).then_inc(memsets_done, 1)
            nc.vector.memset(pick_f[:], 0.0).then_inc(memsets_done, 1)
            dve.wait_ge(memsets_done, 4)
            for e in range(2):
                nc.vector.memset(pick_f[:, e, e:e + 1], 1.0).then_inc(memsets_done, 1)
            dve.wait_ge(memsets_done, 6)
            nc.vector.tensor_copy(pick_row[:], pick_f[:]).then_inc(consts_done, 1)
            def weight_parts():
                dve.wait_ge(consts_loaded, 64)
                nc.vector.tensor_copy(w_hi[:], w_t[:]).then_inc(consts_done, 1)
                dve.wait_ge(consts_done, 2)
                nc.vector.tensor_tensor(w_lo[:], w_t[:], w_hi[:].bitcast(F32), ALU.subtract).then_inc(consts_done, 1)
                for e in range(2):
                    nc.vector.tensor_scalar(b1_ninth[:, :, e], bias1[:], 1.0 / DEG, None, ALU.mult
                                            ).then_inc(consts_done, 1)
                    nc.vector.tensor_scalar(b1_8ninth[:, :, e], bias1[:], TOP / DEG, None, ALU.mult
                                            ).then_inc(consts_done, 1)
                    nc.vector.tensor_copy(b2_pair[:, :, e], bias2[:]).then_inc(consts_done, 1)
                dve.wait_ge(consts_done, 9)

            def step(s):
                if s.k % 2 == 0:
                    if s.has(3, B) and s.k <= 0:
                        low_h(s, 1)
                    if s.has(4, B):
                        bn(s, 4)
                    if s.has(5, B):
                        bn(s, 5)
                    if s.has(0, B):
                        fix(s)
                        second_bias(s)
                    if s.has(3, B) and s.k > 0:
                        low_h(s, 1)
                    if s.has(-1, B):
                        dve.wait_ge(q["out_bias_ready"], s.pair(-2, plus=1))
                        out_half(s, 0)
                        out_half(s, 1)
                    if s.has(0, B):
                        low_r(s, 0)
                        low_r(s, 1)
                else:
                    if s.k == -3:
                        weight_parts()
                    if s.has(1, B):
                        rows_top(s)
                    if s.has(3, B):
                        low_h(s, 0)
                    if s.has(0, B):
                        fix(s)
                    if s.has(-1, B):
                        dve.wait_ge(q["out_bias_ready"], s.pair(-1, plus=1))
                        out_half(s, 0)
                    if s.has(1, B):
                        sum_top(s)
                    if s.has(-1, B):
                        out_half(s, 1)
                    if s.has(1, B):
                        small_vectors(s)
                    if s.has(0, B):
                        low_r(s, 0)
                        low_r(s, 1)

            run_steps(dve, step)
            dve.wait_ge(q["flags_ready"], B // 2)
            nc.vector.tensor_reduce(least_signs[0:2], flags[0:2], AX.X, ALU.min).then_inc(q["least_steps"], 1)
            dve.wait_ge(q["least_steps"], 1)
            nc.vector.tensor_scalar(least[0:2], least_signs[0:2], N - 0.5, None, ALU.is_lt
                                    ).then_inc(q["least_ready"], 1)
            general_vector(dve)

        @block.tensor
        def _(pe):
            def product(hi, lo, sem_done, before, ready=None):
                for m in range(C):
                    before(m)
                    for c in range(C):
                        if m == 0 and ready:
                            ready(c)
                        for w, y in ((w_lo, hi), (w_hi, lo), (w_hi, hi)):
                            for nh in range(NH):
                                u = m * NH + nh
                                end = c == C - 1 and w is w_hi and y is hi
                                mm = nc.tensor.matmul(ps_main[:, u * HALF:(u + 1) * HALF],
                                                      w[:, c, m * P:(m + 1) * P],
                                                      y[:, c, nh * HALF:(nh + 1) * HALF],
                                                      start=(c == 0 and w is w_lo), stop=end)
                                if end:
                                    mm.then_inc(q[sem_done], 1)

            pe.wait_ge(consts_loaded, 64)
            pe.wait_ge(consts_done, 9)

            def step(s):
                odd = s.k % 2 == 1
                loop = not isinstance(s.turn, int)
                def banks1(m):
                    if loop or s.k >= 2:
                        pe.wait_ge(q["out_done"], s.val(U, -2, (m + 1) * NH))
                    elif s.k == 1:
                        pe.wait_ge(q["r_made"], s.val(U, -1, (m + 1) * NH))

                if s.k == -1:
                    product(h_hi[:, 0], h_lo[:, 0], "m1_done", banks1)
                elif s.has(0, B) and (loop or s.k > 0):
                    sl = s.k % HS
                    product(h_hi[:, sl], h_lo[:, sl], "m1_done", banks1)
                if not odd and s.has(0, B):
                    g = s.k // 2 % 2
                    pe.wait_ge(q["r8_ready"], s.pair(0, plus=1))
                    for m in range(C):
                        for c in range(C):
                            last = nc.tensor.matmul(ps_c2[:, 2 * m:2 * m + 2], w_t[:, c, m * P:(m + 1) * P],
                                                    r8[:, g, c, :], start=(c == 0), stop=(c == C - 1))
                    last.then_inc(q["c2_ready"], 1)
                if s.has(-1, B):
                    def banks2(m):
                        if s.has(0, B):
                            pe.wait_ge(q["r_made"], s.val(U, 0, (m + 1) * NH))
                        else:
                            pe.wait_ge(q["out_done"], s.val(U, -2, (m + 1) * NH))

                    def parts2(c):
                        pe.wait_ge(q["r_lo_ready"], s.val(C, -1, c + 1))
                    product(r_hi, r_lo, "m2_done", banks2, parts2)
                if not odd and s.has(2, B):
                    pe.wait_ge(q["h_lo_vec"], s.pair(2, 2, 2))
                    pe.wait_ge(q["h_lo_pool"], s.pair(2, 2, 2))
                    if loop or s.k + 2 >= 2:
                        pe.wait_ge(q["fv_copied"], s.pair(2))
                    terms = [(e, c, y) for e in range(2) for c in range(C) for y in (h_lo, h_hi)]
                    for n, (e, c, y) in enumerate(terms):
                        for nh in range(NH):
                            last = nc.tensor.matmul(ps_fv[:, nh * HALF:(nh + 1) * HALF], pick_row[:, e, :],
                                                    y[:, (s.k + 2 + e) % HS, c, nh * HALF:(nh + 1) * HALF],
                                                    start=(n == 0), stop=(n == len(terms) - 1))
                    last.then_inc(q["fv_ready"], 1)
                if odd and s.has(1, B):
                    sl = (s.k + 1) % HS
                    pe.wait_ge(q["top_summed"], s.pair(1, plus=1))
                    if loop or s.k >= 1:
                        pe.wait_ge(q["top_relued"], s.val(C, 0, C))
                    for m in range(C):
                        for c in range(C):
                            last = nc.tensor.matmul(ps_top[:, 2 * m * COLS:2 * (m + 1) * COLS],
                                                    w_t[:, c, m * P:(m + 1) * P], top_h[:, sl:sl + 2, c, :],
                                                    start=(c == 0), stop=(c == C - 1))
                    last.then_inc(q["top_ready"], 1)

            run_steps(pe, step)
            general_tensor(pe)


def kernel(x, adj, L0_gnn_b1, L0_gnn_b2):
    import numpy as np
    import concourse.bacc as bacc
    from concourse.bass_utils import run_bass_kernel_spmd as run

    nc = bacc.Bacc("TRN2", target_bir_lowering=False, num_devices=1)
    arrays = {
        "x_in": np.ascontiguousarray(x),
        "w_t_in": np.ascontiguousarray(np.asarray(adj).T),
        "b1_in": np.ascontiguousarray(np.asarray(L0_gnn_b1).reshape(-1, P).T),
        "b2_in": np.ascontiguousarray(np.asarray(L0_gnn_b2).reshape(-1, P).T),
        "ident_in": np.eye(P, dtype=np.float32),
    }
    args = [nc.dram_tensor(k, a.shape, mybir.dt.from_np(a.dtype), kind="ExternalInput").ap() for k, a in arrays.items()]
    out = nc.dram_tensor("out", arrays["x_in"].shape, F32, kind="ExternalOutput").ap()
    gnn_kernel(nc, *args, out)
    r = run(nc, [arrays], core_ids=[0])
    return r.results[0]["out"]
```

```python
from contextlib import ExitStack

import numpy as np

import concourse.bass as bass
from concourse import mybir

ALU = mybir.AluOpType
ACT = mybir.ActivationFunctionType
AX = mybir.AxisListType
F32 = mybir.dt.float32
F32R = mybir.dt.float32r
U32 = mybir.dt.uint32

P = 128
TOP = 8
EPS = 1e-5
HALF = 512
XS = 8
HS = 4


class Step:

    def __init__(self, k, turn=0):
        self.k, self.turn = k, turn

    def has(self, off, batches):
        return not isinstance(self.turn, int) or 0 <= self.k + off < batches

    def val(self, per=1, off=0, plus=0):
        fixed = per * (self.k + off) + plus
        return fixed if isinstance(self.turn, int) else self.turn * (8 * per) + fixed

    def pair(self, off, per=1, plus=0):
        fixed = per * ((self.k + off) // 2) + plus
        return fixed if isinstance(self.turn, int) else self.turn * (4 * per) + fixed

    def round(self, off, plus=0):
        fixed = 16 * ((self.k + off) // XS) + plus
        return fixed if isinstance(self.turn, int) else self.turn * 16 + fixed


def gnn_kernel(nc, x, wT, b1, b2, ident_in, out):
    B, S, N = x.shape
    C = S // P
    T = N // P
    NH = N // HALF
    U = C * NH
    DEG = TOP + 1
    COLS = TOP + 2
    GEN_VEC = 11 + 5 * T

    LEAD, LOOP0, TURNS = 5, 2, (B - 8) // 8
    assert LOOP0 + 8 * TURNS - 1 + LEAD < B and B % 8 == 0

    def run_steps(eng, step):
        for k in range(-LEAD, LOOP0):
            step(Step(k))
        with eng.Fori(0, TURNS) as turn:
            for k in range(LOOP0, LOOP0 + 8):
                step(Step(k, turn))
        for k in range(LOOP0 + 8 * TURNS, B + 2):
            step(Step(k))

    with ExitStack() as ctx:
        def sb(name, shape, dt=F32):
            return ctx.enter_context(nc.sbuf_tensor(name, shape, dt))

        def shared(low, full, shape):
            at = nc.sbuf_base
            both = sb(low, shape, F32R), nc.alloc_sbuf_tensor_at(full, shape, F32, offset=at)
            assert nc.sbuf_base == at + 4 * int(np.prod(shape[1:]))
            return both

        def sem(name):
            return ctx.enter_context(nc.semaphore(name))

        def psum(name, cols):
            return ctx.enter_context(nc.psum_tensor(name, [P, cols], F32))

        ps_main = psum("ps_main", U * HALF)
        ps_fv = psum("ps_fv", N)
        ps_top = psum("ps_top", HALF)
        ps_spare = psum("ps_spare", HALF)

        w_t = sb("w_t", [P, C, S])
        w_hi = sb("w_hi", [P, C, S], F32R)
        w_lo = sb("w_lo", [P, C, S], F32R)
        bias1 = sb("bias1", [P, C])
        bias2 = sb("bias2", [P, C])
        b1_ninth = sb("b1_ninth", [P, C, 2])
        b1_8ninth = sb("b1_8ninth", [P, C, 2])
        ident = sb("ident", [P, P])
        ones = sb("ones", [P, P])
        pick_f = sb("pick_f", [P, 2, P])
        pick_row = sb("pick_row", [P, 2, P], F32R)
        minus_half = sb("minus_half", [P, 2, C])
        x_sb = sb("x_sb", [P, XS, C, N])
        h_hi = sb("h_hi", [P, HS, C, N], F32R)
        h_lo, h_f = shared("h_lo", "h_f", [P, HS, C, N])
        lo_sum = sb("lo_sum", [P, N], F32R)
        r_hi = sb("r_hi", [P, 2, C, N], F32R)
        r_lo, r_f = shared("r_lo", "r_f", [P, 2, C, N])
        stats = sb("stats", [P, 2, C, NH, 6])
        mv = sb("mv", [P, 4, C, 2])
        var_eps = sb("var_eps", [P, 2, C])
        rstd = sb("rstd", [P, 2, 2, C])
        mr = sb("mr", [P, 2, 2, C])
        neg_mr = sb("neg_mr", [P, 2, 2, C])
        top_h = sb("top_h", [P, HS, C, COLS])
        relu_bias = sb("relu_bias", [P, 2, C, 2])
        r8_raw = sb("r8_raw", [P, 2, C, 2])
        r8 = sb("r8", [P, 2, C, 2])
        r8_rest = sb("r8_rest", [P, 2, C, 2])
        relu_top = sb("relu_top", [P, C, TOP])
        top_sum = sb("top_sum", [P, 2, C])
        r_sum = sb("r_sum", [P, 2, C])
        r_rest = sb("r_rest", [P, C])
        rho = sb("rho", [P, 2, C])
        sim = sb("sim", [P, N + TOP])
        sim_rest = sb("sim_rest", [P, N + TOP])
        row_a = sb("row_a", [P, N])
        top1 = sb("top1", [P, TOP])
        drop1 = sb("drop1", [P, TOP])
        top8 = sb("top8", [P, TOP])
        found = sb("found", [P, TOP], U32)
        idx = sb("idx", [P, 2, TOP], U32)
        signs = sb("signs", [P, 2])
        flags = sb("flags", [P, B // 2])
        least_signs = sb("least_signs", [P, 1])
        least = sb("least", [P, 1], U32)
        fv_col = sb("fv_col", [P, T])

        consts_loaded = sem("consts_loaded")
        memsets_done = sem("memsets_done")
        consts_done = sem("consts_done")
        first_loaded = [sem(f"first_loaded{c}") for c in range(C)]
        x_loaded = [sem(f"x_loaded{i}") for i in range(XS)]
        x_stored = [sem(f"x_stored{i}") for i in range(XS)]

        def last_extra(i):
            return 16 * (C - 1) if i == XS - 1 else 0

        names = """bn_done aggr_done first_steps first_ready coef_steps coef_ready h_made h_hi_ready
        h_lo_vec h_lo_pool lo_summed fv_ready fv_copied signed
        top_steps idx_ready gathered top_summed top_ready bias_ready r8_steps r8_ready rest_ready
        top_relued m1_done r_made fix_steps rho_ready scattered r_hi_ready r_lo_ready m2_done out_done
        flags_ready least_steps least_ready vec_fence pool_fence sp_fence
        g_x g_var g_std g_vec g_h g_fv g_pick g_turned g_rows g_deg g_mix g_hw g_hwc g_mixed g_relu g_result g_out
        g_stored""".split()
        q = {n: sem(n) for n in names}

        x_dram = x.rearrange("b (c p) n -> b p c n", p=P)
        out_dram = out.rearrange("b (c p) n -> b p c n", p=P)

        block = ctx.enter_context(nc.Block())

        gx, gh, gr = x_sb[:, 0], x_sb[:, 1], x_sb[:, 2]
        hw_t = x_sb[:, 3].rearrange("p c n -> p (c n)").rearrange("p (t s) -> p t s", t=T)
        pick = x_sb[:, XS - 4:XS].rearrange("p a c n -> p (a c) n")
        mix = h_f[:].rearrange("p a c n -> p (a c) n")
        marked = r_f[:, 0, 0]
        half_banks = [ps_fv[:, 0:HALF], ps_fv[:, HALF:2 * HALF], ps_top[:], ps_spare[:]]

        def load_least(eng):
            eng.wait_ge(q["least_ready"], 1)
            one = eng.value_load(least[0:1, 0:1], min_val=0, max_val=1)
            two = eng.value_load(least[1:2, 0:1], min_val=0, max_val=1)
            general = eng.alloc_register("general")
            eng.reg_mov(general, one + two)
            return general

        def general_sync(sp):
            for i in range(XS):
                sp.wait_ge(x_stored[i], 16 * (B // XS) + last_extra(i))
            with sp.If_ne(load_least(sp), 0):
                with sp.Fori(0, B) as b:
                    sp.dma_start(gx, x_dram[bass.ds(b, 1)].rearrange("b p c n -> p (b c) n")).then_inc(q["g_x"], 16)
                    sp.wait_ge(q["g_out"], b + 1)
                    sp.dma_start(out_dram[bass.ds(b, 1)].rearrange("b p c n -> p (b c) n"), gx
                                 ).then_inc(q["g_stored"], 16)
                    sp.wait_ge(q["g_stored"], 16 * b + 16)
                    sp.sem_inc(q["sp_fence"], 1)

        def general_pool(pool):
            with pool.If_ne(load_least(pool), 0):
                with pool.Fori(0, B) as b:
                    pool.wait_ge(q["g_var"], b + 1)
                    pool.sem_inc(q["pool_fence"], 1)
                    nc.gpsimd.tensor_tensor(rstd[:, 0, 0], var_eps[:, 0], minus_half[:, 0], ALU.pow
                                            ).then_inc(q["g_std"], 1)

        def general_vector(dve):
            with dve.If_ne(load_least(dve), 0):
                with dve.Fori(0, B) as b:
                    base = b * GEN_VEC
                    count = [0]

                    def step(ins):
                        count[0] += 1
                        ins.then_inc(q["g_vec"], 1)
                        dve.wait_ge(q["g_vec"], base + count[0])
                        dve.sem_inc(q["vec_fence"], 1)

                    dve.wait_ge(q["g_x"], 16 * b + 16)
                    for c in range(C):
                        for j in range(NH):
                            step(nc.vector.bn_stats(stats[:, 0, c, j, :], gx[:, c, j * HALF:(j + 1) * HALF]))
                    for c in range(C):
                        step(nc.vector.bn_aggr(mv[:, 0, c, :], stats[:, 0, c, :, :]))
                    nc.vector.tensor_scalar(var_eps[:, 0], mv[:, 0, :, 1], EPS, None, ALU.add
                                            ).then_inc(q["g_var"], 1)
                    dve.wait_ge(q["g_std"], b + 1)
                    for c in range(C):
                        step(nc.vector.tensor_scalar(gh[:, c, :], gx[:, c, :], mv[:, 0, c, 0:1],
                                                     rstd[:, 0, 0, c:c + 1], ALU.subtract, ALU.mult))
                    nc.vector.tensor_scalar(gh, gh, 0.0, None, ALU.max).then_inc(q["g_h"], 1)
                    dve.wait_ge(q["g_fv"], b + 1)
                    step(nc.vector.tensor_copy(row_a[:], ps_main[:, 0:N]))
                    step(nc.vector.tensor_copy(fv_col[:], ps_top[:, 0:T]))
                    for t in range(T):
                        step(nc.vector.tensor_scalar(sim[:, 0:N], row_a[:], fv_col[:, t:t + 1], None, ALU.mult))
                        step(nc.vector.max(top1[:], sim[:, 0:N]))
                        step(nc.vector.tensor_copy(drop1[:, 0:1], top1[:, 0:1]))
                        step(nc.vector.match_replace(out=sim_rest[:], in_to_replace=drop1[:], in_values=sim[:],
                                                     imm_value=-3.0))
                        step(nc.vector.max(top8[:], sim_rest[:, 0:N]))
                        nc.vector.match_replace(out=marked, in_to_replace=top8[:], in_values=sim_rest[:, 0:N],
                                                imm_value=1e30).then_inc(q["g_pick"], 1)
                        dve.wait_ge(q["g_pick"], b * 2 * T + 2 * t + 1)
                        nc.vector.tensor_scalar(pick[:, t, :], marked, 1e30, None, ALU.is_ge
                                                ).then_inc(q["g_pick"], 1)
                    dve.wait_ge(q["g_pick"], b * 2 * T + 2 * T)
                    for u in range(T):
                        dve.wait_ge(q["g_turned"], b * T + u + 1)
                        nc.vector.tensor_tensor(mix[:, u, :], pick[:, u, :], ps_main[:, 0:N], ALU.max
                                                ).then_inc(q["g_rows"], 1)
                        dve.wait_ge(q["g_rows"], b * 2 * T + 2 * u + 1)
                        diagonal = mix[:, u, u * P:(u + 1) * P]
                        nc.vector.tensor_tensor(diagonal, diagonal, ident[:], ALU.max).then_inc(q["g_rows"], 1)
                    dve.wait_ge(q["g_deg"], b + 1)
                    step(nc.vector.reciprocal(row_a[:], ps_fv[:, 0:N]))
                    for t in range(T):
                        nc.vector.tensor_tensor(mix[:, t, :], mix[:, t, :], row_a[:], ALU.mult
                                                ).then_inc(q["g_mix"], 1)
                    for layer in range(2):
                        dve.wait_ge(q["g_hw"], 2 * b + layer + 1)
                        nc.vector.tensor_copy(hw_t.rearrange("p t s -> p (t s)"), ps_main[:]).then_inc(q["g_hwc"], 1)
                        dve.wait_ge(q["g_mixed"], 2 * b + layer + 1)
                        for u in range(U):
                            c, at = u // NH, slice(u % NH * HALF, (u % NH + 1) * HALF)
                            if layer == 0:
                                nc.vector.tensor_scalar(gr[:, c, at], half_banks[u], bias1[:, c:c + 1], 0.0,
                                                        ALU.add, ALU.max).then_inc(q["g_relu"], 1)
                            else:
                                nc.vector.scalar_tensor_tensor(
                                    out=gx[:, c, at], in0=half_banks[u], scalar=bias2[:, c:c + 1], in1=gx[:, c, at],
                                    op0=ALU.add, op1=ALU.add).then_inc(q["g_result"], 1)
                    dve.wait_ge(q["g_result"], b * U + U)
                    dve.sem_inc(q["g_out"], 1)
                    assert count[0] == GEN_VEC

        def general_tensor(pe):
            with pe.If_ne(load_least(pe), 0):
                with pe.Fori(0, B) as b:
                    pe.wait_ge(q["g_h"], b + 1)
                    for nh in range(NH):
                        for c in range(C):
                            nc.tensor.matmul(ps_main[:, nh * HALF:(nh + 1) * HALF], ones[:],
                                             gh[:, c, nh * HALF:(nh + 1) * HALF], start=(c == 0), stop=(c == C - 1))
                    for t in range(T):
                        for c in range(C):
                            last = nc.tensor.matmul(ps_top[:, t:t + 1], gh[:, c, t * P:(t + 1) * P], ones[:, 0:1],
                                                    start=(c == 0), stop=(c == C - 1))
                    last.then_inc(q["g_fv"], 1)
                    pe.wait_ge(q["g_pick"], b * 2 * T + 2 * T)
                    for u in range(T):
                        if u > 0:
                            pe.wait_ge(q["g_rows"], b * 2 * T + 2 * u)
                        for t in range(T):
                            last = nc.tensor.transpose(ps_main[:, t * P:(t + 1) * P],
                                                       pick[:, t, u * P:(u + 1) * P], ident[:])
                        last.then_inc(q["g_turned"], 1)
                    pe.wait_ge(q["g_rows"], b * 2 * T + 2 * T)
                    for nh in range(NH):
                        for t in range(T):
                            last = nc.tensor.matmul(ps_fv[:, nh * HALF:(nh + 1) * HALF], ones[:],
                                                    mix[:, t, nh * HALF:(nh + 1) * HALF],
                                                    start=(t == 0), stop=(t == T - 1))
                    last.then_inc(q["g_deg"], 1)
                    pe.wait_ge(q["g_mix"], b * T + T)
                    for layer, y in ((0, gh), (1, gr)):
                        if layer == 1:
                            pe.wait_ge(q["g_relu"], U * b + U)
                        for t in range(T):
                            for c in range(C):
                                last = nc.tensor.matmul(ps_main[:, t * S:(t + 1) * S], y[:, c, t * P:(t + 1) * P],
                                                        w_t[:, c, :], start=(c == 0), stop=(c == C - 1))
                        last.then_inc(q["g_hw"], 1)
                        pe.wait_ge(q["g_hwc"], 2 * b + layer + 1)
                        for u in range(U):
                            m, nh = u // NH, u % NH
                            for t in range(T):
                                last = nc.tensor.matmul(half_banks[u], hw_t[:, t, m * P:(m + 1) * P],
                                                        mix[:, t, nh * HALF:(nh + 1) * HALF],
                                                        start=(t == 0), stop=(t == T - 1))
                        last.then_inc(q["g_mixed"], 1)

        @block.sync
        def _(sp):
            for c in range(C):
                sp.dma_start(x_sb[:, 0, c], x_dram[0][:, c]).then_inc(first_loaded[c], 16)
            sp.dma_start(x_sb[:, 1], x_dram[1]).then_inc(x_loaded[1], 16)
            sp.dma_start(w_t[:], wT.rearrange("(c p) n -> p c n", p=P)).then_inc(consts_loaded, 16)
            sp.dma_start(bias1[:], b1).then_inc(consts_loaded, 16)
            sp.dma_start(bias2[:], b2).then_inc(consts_loaded, 16)
            sp.dma_start(ident[:], ident_in).then_inc(consts_loaded, 16)
            for i in range(2, XS):
                sp.dma_start(x_sb[:, i], x_dram[i]).then_inc(x_loaded[i], 16)
            with sp.Fori(1, B // XS) as turn:
                for i in range(XS):
                    sp.wait_ge(x_stored[i], turn * 16)
                    sp.dma_start(x_sb[:, i], x_dram[bass.ds(turn * XS + i, 1)].rearrange("b p c n -> p (b c) n")
                                 ).then_inc(x_loaded[i], 16)
            general_sync(sp)

        @block.scalar
        def _(act):
            def copy_sums(s):
                if s.has(1, B):
                    act.wait_ge(q["fv_ready"], s.pair(1, plus=1))
                    nc.scalar.activation(sim[0:2, 0:N], ps_fv[0:2, :], ACT.Copy).then_inc(q["fv_copied"], 1)

            def count_positive(s):
                if s.has(1, B):
                    g = (s.k + 1) // 2 % 2
                    act.wait_ge(q["fv_copied"], s.pair(1, plus=1))
                    nc.scalar.activation(row_a[0:2, :], sim[0:2, 0:N], ACT.Sign,
                                         accum_out=signs[0:2, g:g + 1]).then_inc(q["signed"], 1)

            def norm_h(s, c, off=3):
                if not s.has(off, B):
                    return
                bb = s.k + off
                if s.k == -off:
                    act.wait_ge(q["first_ready"], 1)
                elif c == 0:
                    act.wait_ge(q["coef_ready"], s.pair(off - bb % 2, plus=1))
                nc.scalar.activation(h_f[:, bb % HS, c], x_sb[:, bb % XS, c], ACT.Relu,
                                     bias=neg_mr[:, bb // 2 % 2, bb % 2, c:c + 1],
                                     scale=rstd[:, bb // 2 % 2, bb % 2, c:c + 1],
                                     accum_out=top_h[:, bb % HS, c, COLS - 1:COLS]).then_inc(q["h_made"], 1)

            def high_h(s, c, off=3):
                if s.has(off, B):
                    bb = s.k + off
                    act.wait_ge(q["h_made"], s.val(C, off, c + 1))
                    nc.scalar.activation(h_hi[:, bb % HS, c], h_f[:, bb % HS, c], ACT.Copy
                                         ).then_inc(q["h_hi_ready"], 1)

            def relu_tops(s):
                if s.has(0, B):
                    g, e = s.k // 2 % 2, s.k % 2
                    act.wait_ge(q["bias_ready"], s.pair(-e, plus=1))
                    for m in range(C):
                        nc.scalar.activation(relu_top[:, m], ps_top[:, (2 * m + e) * COLS:(2 * m + e) * COLS + TOP],
                                             ACT.Relu, bias=relu_bias[:, g, m, e:e + 1], scale=1.0 / DEG ** 2,
                                             accum_out=top_sum[:, e, m:m + 1]).then_inc(q["top_relued"], 1)

            def store(s):
                if s.has(-2, B):
                    i = (s.k - 2) % XS
                    if s.k - 2 < B - 1:
                        act.wait_ge(q["out_done"], s.val(C, -2, C))
                        act.dma_start(out_at(s, -2), x_sb[:, i]).then_inc(x_stored[i], 16)
                    else:
                        for m in range(C):
                            act.wait_ge(q["out_done"], s.val(C, -2, m + 1))
                            act.dma_start(out_at(s, -2)[:, m], x_sb[:, i, m]).then_inc(x_stored[i], 16)

            def high_r(s, c):
                if s.has(0, B):
                    g, e = s.k // 2 % 2, s.k % 2
                    if c == 0:
                        act.wait_ge(q["scattered"], s.val(1, 0, 1))
                    nc.scalar.activation(r_hi[:, s.k % 2, c], r_f[:, e, c], ACT.Identity,
                                         bias=r8[:, g, c, e:e + 1], scale=1.0).then_inc(q["r_hi_ready"], 1)

            def relu_half(s, m):
                if not s.has(0, B):
                    return
                g, e = s.k // 2 % 2, s.k % 2
                act.wait_ge(q["m1_done"], s.val(C, 0, m + 1))
                nc.scalar.activation(r_f[:, e, m], ps_main[:, m * N:(m + 1) * N], ACT.Relu,
                                     bias=relu_bias[:, g, m, e:e + 1], scale=1.0 / DEG ** 2,
                                     accum_out=r_sum[:, e, m:m + 1]).then_inc(q["r_made"], 1)

            def out_at(s, off):
                if isinstance(s.turn, int):
                    return out_dram[s.k + off]
                return out_dram[bass.ds(s.val(1, off), 1)].rearrange("b p c n -> p (b c) n")

            def step(s):
                if s.k <= 0:
                    if s.k % 2 == 1:
                        copy_sums(s)
                    for c in range(C):
                        norm_h(s, c)
                        high_h(s, c)
                    relu_tops(s)
                    relu_half(s, 0)
                    relu_half(s, 1)
                    if s.k % 2 == 1:
                        count_positive(s)
                    high_r(s, 0)
                    high_r(s, 1)
                elif s.k % 2 == 0:
                    relu_tops(s)
                    relu_half(s, 0)
                    relu_half(s, 1)
                    norm_h(s, 1)
                    store(s)
                    high_h(s, 1)
                    high_r(s, 0)
                    high_r(s, 1)
                else:
                    copy_sums(s)
                    norm_h(s, 0)
                    relu_tops(s)
                    relu_half(s, 0)
                    high_h(s, 0)
                    relu_half(s, 1)
                    norm_h(s, 1)
                    count_positive(s)
                    store(s)
                    high_h(s, 1)
                    norm_h(s, 0, 4)
                    high_h(s, 0, 4)
                    high_r(s, 0)
                    high_r(s, 1)

            run_steps(act, step)
            for i in range(XS):
                act.wait_ge(x_stored[i], 16 * (B // XS) + last_extra(i))

        @block.gpsimd
        def _(pool):
            def hold(name, value):
                pool.wait_ge(q[name], value)
                pool.sem_inc(q["pool_fence"], 1)

            def load_idx(e, g):
                return nc.values_load_multi_w_load_instructions(
                    idx[e:e + 1, g, :], engines=[mybir.EngineType.Pool], min_val=0, max_val=N - 1,
                    skip_runtime_bounds_check_because="idx is clamped to N - 1 and unsigned")[1]

            nc.gpsimd.memset(minus_half[:], -0.5).then_inc(q["pool_fence"], 1)
            pool.wait_ge(q["pool_fence"], 1)

            def low_h(s, c):
                if not s.has(3, B):
                    return
                bb = s.k + 3
                pool.wait_ge(q["h_hi_ready"], s.val(C, 3, c + 1))
                nc.gpsimd.tensor_tensor(h_lo[:, bb % HS, c], h_f[:, bb % HS, c], h_hi[:, bb % HS, c].bitcast(F32),
                                        ALU.subtract).then_inc(q["h_lo_pool"], 1)

            def sum_low(s):
                if s.k < 1 or not s.has(3, B):
                    return
                slot = (s.k + 3) % HS
                pool.wait_ge(q["h_lo_vec"], s.val(1, 3, 1))
                pool.wait_ge(q["h_lo_pool"], s.val(1, 3, 1))
                pool.wait_ge(q["fv_ready"], s.pair(1, plus=1))
                nc.gpsimd.tensor_tensor(lo_sum[:], h_lo[:, slot, 0].bitcast(F32), h_lo[:, slot, 1].bitcast(F32),
                                        ALU.add).then_inc(q["lo_summed"], 1)

            def coefficient_steps(steps, ready, before, j, es, at):
                nc.gpsimd.tensor_scalar(var_eps[:, es], mv[:, at, :, 1], EPS, None, ALU.add).then_inc(q[steps], 1)
                hold(steps, before(1))
                nc.gpsimd.tensor_tensor(rstd[:, j, es], var_eps[:, es], minus_half[:, es], ALU.pow
                                        ).then_inc(q[steps], 1)
                hold(steps, before(2))
                nc.gpsimd.tensor_tensor(mr[:, j, es], mv[:, at, :, 0], rstd[:, j, es], ALU.mult
                                        ).then_inc(q[steps], 1)
                hold(steps, before(3))
                nc.gpsimd.tensor_scalar(neg_mr[:, j, es], mr[:, j, es], -1.0, None, ALU.mult).then_inc(q[ready], 1)

            def coefficients(s):
                if not s.has(4, B):
                    return
                first, at = int(s.k == -LEAD + 1), (s.k + 4) % 4
                hold("aggr_done", s.pair(4, 2 * C, 2 * C))
                coefficient_steps("coef_steps", "coef_ready", lambda n: s.pair(4, 3, n), (s.k + 4) // 2 % 2,
                                  slice(first, 2), slice(at + first, at + 2))

            def gather(s):
                if not s.has(1, B):
                    return
                g = (s.k + 1) // 2 % 2
                hold("idx_ready", s.pair(1, plus=1))
                for e in range(2):
                    sl = (s.k + 1 + e) % HS
                    for t, v in enumerate(load_idx(e, g)):
                        last = nc.gpsimd.tensor_tensor(
                            top_h[:, sl, :, t:t + 1], h_hi[:, sl, :, bass.ds(v, 1)].bitcast(F32),
                            h_lo[:, sl, :, bass.ds(v, 1)].bitcast(F32), ALU.add)
                last.then_inc(q["gathered"], 1)

            def scatter(s):
                if not s.has(0, B):
                    return
                nodes = load_idx(s.k % 2, s.k // 2 % 2)
                hold("rho_ready", s.val(1, 0, 1))
                for v in nodes:
                    last = nc.gpsimd.tensor_copy(r_f[:, s.k % 2, :, bass.ds(v, 1)],
                                                 rho[:, s.k % 2, :].rearrange("p (c o) -> p c o", o=1))
                last.then_inc(q["scattered"], 1)

            def keep_flag(s):
                if not s.has(1, B):
                    return
                g = (s.k + 1) // 2 % 2
                hold("signed", s.pair(1, plus=1))
                at = s.pair(1)
                spot = flags[0:2, at:at + 1] if isinstance(s.turn, int) else flags[0:2, bass.ds(at, 1)]
                nc.gpsimd.tensor_copy(spot, signs[0:2, g:g + 1]).then_inc(q["flags_ready"], 1)

            def step(s):
                if s.k % 2 == 0:
                    low_h(s, 0)
                    scatter(s)
                    coefficients(s)
                else:
                    gather(s)
                    scatter(s)
                    low_h(s, 1)
                    sum_low(s)
                    keep_flag(s)

            hold("aggr_done", C)
            coefficient_steps("first_steps", "first_ready", lambda n: n, 0, slice(0, 1), slice(0, 1))
            run_steps(pool, step)
            general_pool(pool)

        @block.vector
        def _(dve):
            def hold(name, value):
                dve.wait_ge(q[name], value)
                dve.sem_inc(q["vec_fence"], 1)

            def rows_top(s):
                if not s.has(1, B):
                    bn(s, 5, 0)
                    return
                between = [0, 1] if s.k >= 1 else []
                g = (s.k + 1) // 2 % 2
                hold("fv_copied", s.pair(1, plus=1))
                nc.vector.max(top1[0:2], sim[0:2, 0:N]).then_inc(q["top_steps"], 1)
                bn(s, 5, 0, between[:1])
                hold("top_steps", s.pair(1, 5, 1))
                nc.vector.tensor_copy(drop1[0:2, 0:1], top1[0:2, 0:1]).then_inc(q["top_steps"], 1)
                hold("top_steps", s.pair(1, 5, 2))
                nc.vector.match_replace(out=sim_rest[0:2], in_to_replace=drop1[0:2], in_values=sim[0:2],
                                        imm_value=-3.0).then_inc(q["top_steps"], 1)
                bn(s, 5, 0, between[1:])
                hold("top_steps", s.pair(1, 5, 3))
                nc.vector.max(top8[0:2], sim_rest[0:2, 0:N]).then_inc(q["top_steps"], 1)
                hold("top_steps", s.pair(1, 5, 4))
                nc.vector.max_index(found[0:2], top8[0:2], sim_rest[0:2, 0:N]).then_inc(q["top_steps"], 1)
                hold("top_steps", s.pair(1, 5, 5))
                nc.vector.tensor_scalar(idx[0:2, g, :], found[0:2], N - 1, None, ALU.min).then_inc(q["idx_ready"], 1)
                if not between:
                    bn(s, 5, 0)

            def bn(s, off, c, halves=range(NH)):
                if not s.has(off, B):
                    return
                i, e = (s.k + off) % XS, (s.k + off) % 2
                if s.k + off == 0:
                    dve.wait_ge(first_loaded[c], 16)
                else:
                    dve.wait_ge(x_loaded[i], s.round(off, 16 if i > 0 else 0))
                for j in halves:
                    nc.vector.bn_stats(stats[:, e, c, j, :], x_sb[:, i, c, j * HALF:(j + 1) * HALF]
                                       ).then_inc(q["bn_done"], 1)

            def bn_end(s, off):
                if s.has(off, B):
                    hold("bn_done", s.val(C * NH, off, C * NH))
                    for c in range(C):
                        nc.vector.bn_aggr(mv[:, (s.k + off) % 4, c, :], stats[:, (s.k + off) % 2, c, :, :]
                                          ).then_inc(q["aggr_done"], 1)

            def fix(s):
                if not s.has(0, B):
                    return
                e, g = s.k % 2, s.k // 2 % 2
                dve.wait_ge(q["r_made"], s.val(C, 0, C))
                nc.vector.tensor_tensor(r_rest[:], r_sum[:, e, :], top_sum[:, e, :], ALU.subtract
                                        ).then_inc(q["fix_steps"], 1)
                dve.wait_ge(q["fix_steps"], s.val(1, 0, 1))
                dve.wait_ge(q["rest_ready"], s.pair(-1 if s.k % 2 else 0, plus=1))
                nc.vector.scalar_tensor_tensor(out=rho[:, e, :], in0=r_rest[:], scalar=DEG / N,
                                               in1=r8_rest[:, g, :, e], op0=ALU.mult, op1=ALU.add
                                               ).then_inc(q["rho_ready"], 1)

            def out_half(s, m):
                if not s.has(-1, B):
                    return
                i = (s.k - 1) % XS
                part = x_sb[:, i, m]
                dve.wait_ge(q["m2_done"], s.val(C, -1, m + 1))
                nc.vector.scalar_tensor_tensor(out=part, in0=ps_main[:, m * N:(m + 1) * N], scalar=bias2[:, m:m + 1],
                                               in1=part, op0=ALU.add, op1=ALU.add).then_inc(q["out_done"], 1)

            def low_h(s, c):
                if not s.has(3, B):
                    return
                bb = s.k + 3
                dve.wait_ge(q["h_hi_ready"], s.val(C, 3, c + 1))
                nc.vector.tensor_tensor(h_lo[:, bb % HS, c], h_f[:, bb % HS, c], h_hi[:, bb % HS, c].bitcast(F32),
                                        ALU.subtract).then_inc(q["h_lo_vec"], 1)

            def low_r(s, c):
                if not s.has(0, B):
                    return
                dve.wait_ge(q["r_hi_ready"], s.val(C, 0, c + 1))
                nc.vector.scalar_tensor_tensor(out=r_lo[:, s.k % 2, c], in0=r_f[:, s.k % 2, c],
                                               scalar=r8[:, s.k // 2 % 2, c, s.k % 2:s.k % 2 + 1],
                                               in1=r_hi[:, s.k % 2, c].bitcast(F32), op0=ALU.add, op1=ALU.subtract
                                               ).then_inc(q["r_lo_ready"], 1)

            def sum_top(s):
                if not s.has(1, B):
                    return
                sl = (s.k + 1) % HS
                dve.wait_ge(q["gathered"], s.pair(1, plus=1))
                nc.vector.tensor_reduce(top_h[:, sl:sl + 2, :, TOP], top_h[:, sl:sl + 2, :, 0:TOP], AX.X, ALU.add
                                        ).then_inc(q["top_summed"], 1)

            def small_vectors(s):
                if not s.has(1, B):
                    return
                g = (s.k + 1) // 2 % 2
                small = ps_top[:, 0:2 * C * COLS].rearrange("p (m e k) -> p m e k", m=C, e=2)
                dve.wait_ge(q["top_ready"], s.pair(1, plus=1))
                nc.vector.scalar_tensor_tensor(out=r8_raw[:, g], in0=small[:, :, :, TOP + 1], scalar=TOP / DEG / N,
                                               in1=b1_8ninth[:], op0=ALU.mult, op1=ALU.add).then_inc(q["r8_steps"], 1)
                nc.vector.scalar_tensor_tensor(out=relu_bias[:, g], in0=small[:, :, :, TOP], scalar=1.0 / DEG ** 2,
                                               in1=b1_ninth[:], op0=ALU.mult, op1=ALU.add
                                               ).then_inc(q["bias_ready"], 1)
                dve.wait_ge(q["r8_steps"], s.pair(1, 1, 1))
                nc.vector.tensor_scalar(r8[:, g], r8_raw[:, g], 0.0, None, ALU.max).then_inc(q["r8_ready"], 1)
                dve.wait_ge(q["r8_ready"], s.pair(1, plus=1))
                nc.vector.tensor_scalar(r8_rest[:, g], r8[:, g], DEG / N - 1.0, None, ALU.mult
                                        ).then_inc(q["rest_ready"], 1)

            nc.vector.memset(ones[:], 1.0).then_inc(memsets_done, 1)
            nc.vector.memset(sim[:, N:], -2.0).then_inc(memsets_done, 1)
            nc.vector.memset(drop1[:], -2.0).then_inc(memsets_done, 1)
            nc.vector.memset(pick_f[:], 0.0).then_inc(memsets_done, 1)
            dve.wait_ge(memsets_done, 4)
            for e in range(2):
                nc.vector.memset(pick_f[:, e, e:e + 1], 1.0).then_inc(memsets_done, 1)
            dve.wait_ge(memsets_done, 6)
            nc.vector.tensor_copy(pick_row[:], pick_f[:]).then_inc(consts_done, 1)

            def weight_parts():
                dve.wait_ge(consts_loaded, 64)
                nc.vector.tensor_copy(w_hi[:], w_t[:]).then_inc(consts_done, 1)
                dve.wait_ge(consts_done, 2)
                nc.vector.tensor_tensor(w_lo[:], w_t[:], w_hi[:].bitcast(F32), ALU.subtract).then_inc(consts_done, 1)
                for e in range(2):
                    nc.vector.tensor_scalar(b1_ninth[:, :, e], bias1[:], 1.0 / DEG, None, ALU.mult
                                            ).then_inc(consts_done, 1)
                    nc.vector.tensor_scalar(b1_8ninth[:, :, e], bias1[:], TOP / DEG, None, ALU.mult
                                            ).then_inc(consts_done, 1)
                dve.wait_ge(consts_done, 7)

            def step(s):
                if s.k <= 0 and s.k % 2 == 0:
                    low_h(s, 1)
                    fix(s)
                    bn(s, 5, 0)
                    bn(s, 5, 1)
                    bn_end(s, 5)
                    low_r(s, 0)
                    low_r(s, 1)
                elif s.k % 2 == 0:
                    bn(s, 5, 0)
                    bn(s, 5, 1)
                    bn_end(s, 5)
                    fix(s)
                    low_h(s, 1)
                    out_half(s, 0)
                    out_half(s, 1)
                    low_r(s, 0)
                    low_r(s, 1)
                elif s.k >= B - 1:
                    fix(s)
                    out_half(s, 0)
                    low_r(s, 0)
                    low_r(s, 1)
                    out_half(s, 1)
                else:
                    if s.k == -3:
                        weight_parts()
                    rows_top(s)
                    out_half(s, 0)
                    fix(s)
                    low_h(s, 0)
                    sum_top(s)
                    out_half(s, 1)
                    small_vectors(s)
                    bn(s, 5, 1)
                    bn_end(s, 5)
                    low_r(s, 0)
                    low_r(s, 1)

            run_steps(dve, step)
            dve.wait_ge(q["flags_ready"], B // 2)
            nc.vector.tensor_reduce(least_signs[0:2], flags[0:2], AX.X, ALU.min).then_inc(q["least_steps"], 1)
            dve.wait_ge(q["least_steps"], 1)
            nc.vector.tensor_scalar(least[0:2], least_signs[0:2], N - 0.5, None, ALU.is_lt
                                    ).then_inc(q["least_ready"], 1)
            general_vector(dve)

        @block.tensor
        def _(pe):
            def product(hi, lo, sem_done, before, ready=None, early=None):
                for m in range(C):
                    before(m)
                    for c in range(C):
                        if m == 0 and ready:
                            ready(c)
                        for w, y in ((w_lo, hi), (w_hi, lo), (w_hi, hi)):
                            for nh in range(NH):
                                u = m * NH + nh
                                end = c == C - 1 and w is w_hi and y is hi
                                mm = nc.tensor.matmul(ps_main[:, u * HALF:(u + 1) * HALF],
                                                      w[:, c, m * P:(m + 1) * P],
                                                      y[:, c, nh * HALF:(nh + 1) * HALF],
                                                      start=(c == 0 and w is w_lo), stop=end)
                                if end and nh == NH - 1:
                                    mm.then_inc(q[sem_done], 1)
                        if m == 0 and c == 0 and early:
                            early()

            def top_product(s, off):
                sl = (s.k + off) % HS
                pe.wait_ge(q["top_summed"], s.pair(off, plus=1))
                if s.k + off >= 2:
                    pe.wait_ge(q["top_relued"], s.val(C, off - 1, C))
                for m in range(C):
                    for c in range(C):
                        last = nc.tensor.matmul(ps_top[:, 2 * m * COLS:2 * (m + 1) * COLS],
                                                w_t[:, c, m * P:(m + 1) * P], top_h[:, sl:sl + 2, c, :],
                                                start=(c == 0), stop=(c == C - 1))
                last.then_inc(q["top_ready"], 1)

            pe.wait_ge(consts_loaded, 64)
            pe.wait_ge(consts_done, 7)

            def step(s):
                odd = s.k % 2 == 1
                loop = not isinstance(s.turn, int)

                def banks1(m):
                    if loop or s.k >= 2:
                        pe.wait_ge(q["out_done"], s.val(C, -2, m + 1))
                    elif s.k == 1:
                        pe.wait_ge(q["r_made"], s.val(C, -1, m + 1))

                if s.k == -1:
                    product(h_hi[:, 0], h_lo[:, 0], "m1_done", banks1)
                elif s.has(0, B) and (loop or s.k > 0):
                    sl = s.k % HS
                    product(h_hi[:, sl], h_lo[:, sl], "m1_done", banks1,
                            early=None if odd else lambda: top_product(s, 0))
                if s.has(-1, B):
                    def banks2(m):
                        if s.has(0, B):
                            pe.wait_ge(q["r_made"], s.val(C, 0, m + 1))
                        else:
                            pe.wait_ge(q["out_done"], s.val(C, -2, m + 1))

                    def parts2(c):
                        pe.wait_ge(q["r_lo_ready"], s.val(C, -1, c + 1))
                    product(r_hi[:, (s.k - 1) % 2], r_lo[:, (s.k - 1) % 2], "m2_done", banks2, parts2)
                if not odd and s.has(2, B):
                    if s.k >= 0:
                        pe.wait_ge(q["fv_copied"], s.pair(2))
                    terms = []
                    for e in range(2):
                        slot, summed = (s.k + 2 + e) % HS, e == 0 and s.k >= 2
                        lows = [lo_sum[:]] if summed else [h_lo[:, slot, c] for c in range(C)]
                        ready = "hi", "sum" if summed else "lo"
                        terms += [(e, ready[0] if c == 0 else "", h_hi[:, slot, c]) for c in range(C)]
                        terms += [(e, ready[1] if n == 0 else "", y) for n, y in enumerate(lows)]
                    for n, (e, first, y) in enumerate(terms):
                        if first == "hi":
                            pe.wait_ge(q["h_hi_ready"], s.val(C, 2 + e, C))
                        elif first == "sum":
                            pe.wait_ge(q["lo_summed"], s.pair(0))
                        elif first == "lo":
                            pe.wait_ge(q["h_lo_vec"], s.val(1, 2 + e, 1))
                            pe.wait_ge(q["h_lo_pool"], s.val(1, 2 + e, 1))
                        for nh in range(NH):
                            last = nc.tensor.matmul(ps_fv[:, nh * HALF:(nh + 1) * HALF], pick_row[:, e, :],
                                                    y[:, nh * HALF:(nh + 1) * HALF],
                                                    start=(n == 0), stop=(n == len(terms) - 1))
                    last.then_inc(q["fv_ready"], 1)
                if s.k == -1:
                    top_product(s, 1)

            run_steps(pe, step)
            general_tensor(pe)


def kernel(x, adj, L0_gnn_b1, L0_gnn_b2):
    import numpy as np
    import concourse.bacc as bacc
    from concourse.bass_utils import run_bass_kernel_spmd as run

    nc = bacc.Bacc("TRN2", target_bir_lowering=False, num_devices=1)
    arrays = {
        "x_in": np.ascontiguousarray(x),
        "w_t_in": np.ascontiguousarray(np.asarray(adj).T),
        "b1_in": np.ascontiguousarray(np.asarray(L0_gnn_b1).reshape(-1, P).T),
        "b2_in": np.ascontiguousarray(np.asarray(L0_gnn_b2).reshape(-1, P).T),
        "ident_in": np.eye(P, dtype=np.float32),
    }
    args = [nc.dram_tensor(k, a.shape, mybir.dt.from_np(a.dtype), kind="ExternalInput").ap() for k, a in arrays.items()]
    out = nc.dram_tensor("out", arrays["x_in"].shape, F32, kind="ExternalOutput").ap()
    gnn_kernel(nc, *args, out)
    r = run(nc, [arrays], core_ids=[0])
    return r.results[0]["out"]
```
